# Optimizing a Trainium2 kernel written in Bass

```python
import numpy as np
import jax
import jax.numpy as jnp

def _softmax(x, axis=-1):
    return jax.nn.softmax(x, axis=axis)

def _gelu(x):
    return jax.nn.gelu(x, approximate=True)

def _silu(x):
    return jax.nn.silu(x)

def _sigmoid(x):
    return jax.nn.sigmoid(x)

def _layernorm(x, axis=-1, eps=1e-05):
    m = jnp.mean(x, axis=axis, keepdims=True)
    v = jnp.var(x, axis=axis, keepdims=True)
    return (x - m) / jnp.sqrt(v + eps)

def _scatter_add(tgt, idx, src, axis=0):
    return tgt.at[idx].add(src)

def _segment_sum(src, seg, n):
    return jax.ops.segment_sum(src, seg, n)
kernel_name = 'mk_cond_seq_d2_seqx_r8_b85f6e'

def setup_inputs(seed: int=0):
    np.random.seed(seed)
    _w = jnp.asarray

    def _rec_inputs():
        import jax
        import jax.numpy as jnp
        _rk = jax.random.key(seed)
        x = -0.000125 + 0.9999 * jax.random.normal(jax.random.fold_in(_rk, 1), (8, 256, 128), jnp.float32)
        _lenS = 256 - jax.random.randint(jax.random.fold_in(_rk, 7), (8,), 0, max(1, 256 // 4) + 1, jnp.int32)
        _lenS2 = 256 - jax.random.randint(jax.random.fold_in(_rk, 8), (8,), 0, max(1, 256 // 4) + 1, jnp.int32)
        itok_B_0_15 = jax.random.randint(jax.random.fold_in(_rk, 11), (8,), 0, 16, jnp.int32)
        itok_B_6_14 = jax.random.randint(jax.random.fold_in(_rk, 12), (8,), 6, 15, jnp.int32)
        return (x, itok_B_0_15, itok_B_6_14)
    x, itok_B_0_15, itok_B_6_14 = _rec_inputs()

    def _L0_cond_setup():
        import jax, jax.numpy as jnp
        import numpy as np
        B, S, D = (32, 128, 128)
        A = 32
        E = 16
        LN_EPS = 1e-05
        key = jax.random.key(seed)
        ks = jax.random.split(key, 10)
        s = lambda fan_in: 1.0 / np.sqrt(fan_in)
        return {'hidden_states': jax.random.normal(ks[0], (B, S, D), dtype=jnp.float32), 'domain_id': jax.random.randint(ks[1], (B,), 0, E, dtype=jnp.int64), 'down_W': jax.random.uniform(ks[2], (A, D), jnp.float32, -s(D), s(D)), 'down_b': jax.random.uniform(ks[3], (A,), jnp.float32, -s(D), s(D)), 'up_W': jax.random.uniform(ks[4], (D, A), jnp.float32, -s(A), s(A)), 'up_b': jax.random.uniform(ks[5], (D,), jnp.float32, -s(A), s(A)), 'expert_W': jax.random.uniform(ks[6], (E, A, A), jnp.float32, -s(A), s(A)), 'expert_b': jax.random.uniform(ks[7], (E, A), jnp.float32, -s(A), s(A)), 'domain_emb': jax.random.normal(ks[8], (E, A), dtype=jnp.float32), 'ln_gamma': jnp.ones((D,), jnp.float32), 'ln_beta': jnp.zeros((D,), jnp.float32)}
    _L0_cond_all = _L0_cond_setup()
    _L0_cond_in = {k: v for k, v in _L0_cond_all.items() if k in ('down_W', 'down_b', 'up_W', 'up_b', 'expert_W', 'expert_b', 'domain_emb', 'ln_gamma', 'ln_beta')}
    del _L0_cond_all

    def _L1_cond_setup():
        import jax, jax.numpy as jnp
        import numpy as np
        D = 128
        E = 8
        FF = 512
        TOPK = 2
        S = 32
        SE = 64
        SH = 128
        B, T = (2, 256)

        def _forward(x, subject_ids, ln_g, ln_b, subj_emb, hyp_w1, hyp_b1, hyp_w2, hyp_b2, sty_w1, sty_b1, sty_w2, sty_b2, router_w, exp_w1, exp_b1, exp_w2, exp_b2):
            mu = x.mean(-1, keepdims=True)
            var = x.var(-1, keepdims=True)
            h = (x - mu) * jax.lax.rsqrt(var + 1e-05) * ln_g + ln_b
            m_t = h.mean(1, keepdims=True)
            v_t = h.var(1, keepdims=True)
            h_norm = (h - m_t) * jax.lax.rsqrt(v_t + 1e-08)
            se = subj_emb[subject_ids]
            hyp = jax.nn.relu(se @ hyp_w1 + hyp_b1) @ hyp_w2 + hyp_b2
            sty = jax.nn.relu(hyp @ sty_w1 + sty_b1) @ sty_w2 + sty_b2
            gamma, beta = jnp.split(sty, 2, axis=-1)
            gamma = jax.nn.softplus(gamma) + 1e-08
            h = h_norm * gamma[:, None, :] + beta[:, None, :]
            h_flat = h.reshape(-1, D)
            probs = jax.nn.softmax(h_flat @ router_w, axis=-1)
            gates, idx = jax.lax.top_k(probs, TOPK)
            gates = gates / gates.sum(-1, keepdims=True)
            N = h_flat.shape[0]
            combine = jnp.zeros((N, E), h_flat.dtype).at[jnp.arange(N)[:, None], idx].add(gates)
            hid = jax.nn.relu(jnp.einsum('nd,edf->nef', h_flat, exp_w1) + exp_b1)
            eout = jnp.einsum('nef,efd->ned', hid, exp_w2) + exp_b2
            y = jnp.einsum('ned,ne->nd', eout, combine)
            return x + y.reshape(x.shape)
        key = jax.random.key(seed)
        ks = jax.random.split(key, 16)
        n = lambda k, sh, s=0.02: jax.random.normal(k, sh, dtype=jnp.float32) * s
        return {'x': jax.random.normal(ks[0], (B, T, D), dtype=jnp.float32), 'subject_ids': jax.random.randint(ks[1], (B,), 0, S), 'ln_g': jnp.ones((D,), jnp.float32), 'ln_b': jnp.zeros((D,), jnp.float32), 'subj_emb': n(ks[2], (S, SE)), 'hyp_w1': n(ks[3], (SE, SH), 1.0 / np.sqrt(SE)), 'hyp_b1': jnp.zeros((SH,), jnp.float32), 'hyp_w2': n(ks[4], (SH, SH), 1.0 / np.sqrt(SH)), 'hyp_b2': jnp.zeros((SH,), jnp.float32), 'sty_w1': n(ks[5], (SH, SH // 2), 1.0 / np.sqrt(SH)), 'sty_b1': jnp.zeros((SH // 2,), jnp.float32), 'sty_w2': n(ks[6], (SH // 2, 2 * D), 1.0 / np.sqrt(SH // 2)), 'sty_b2': jnp.zeros((2 * D,), jnp.float32), 'router_w': n(ks[7], (D, E), 1.0 / np.sqrt(D)), 'exp_w1': n(ks[8], (E, D, FF), 1.0 / np.sqrt(D)), 'exp_b1': jnp.zeros((E, FF), jnp.float32), 'exp_w2': n(ks[9], (E, FF, D), 1.0 / np.sqrt(FF)), 'exp_b2': jnp.zeros((E, D), jnp.float32)}
    _L1_cond_all = _L1_cond_setup()
    _L1_cond_in = {k: v for k, v in _L1_cond_all.items() if k in ('ln_g', 'ln_b', 'subj_emb', 'hyp_w1', 'hyp_b1', 'hyp_w2', 'hyp_b2', 'sty_w1', 'sty_b1', 'sty_w2', 'sty_b2', 'router_w', 'exp_w1', 'exp_b1', 'exp_w2', 'exp_b2')}
    del _L1_cond_all
    return {'x': x, 'itok_B_0_15': itok_B_0_15, 'itok_B_6_14': itok_B_6_14, 'L0_cond_down_W': _L0_cond_in['down_W'], 'L0_cond_down_b': _L0_cond_in['down_b'], 'L0_cond_up_W': _L0_cond_in['up_W'], 'L0_cond_up_b': _L0_cond_in['up_b'], 'L0_cond_expert_W': _L0_cond_in['expert_W'], 'L0_cond_expert_b': _L0_cond_in['expert_b'], 'L0_cond_domain_emb': _L0_cond_in['domain_emb'], 'L0_cond_ln_gamma': _L0_cond_in['ln_gamma'], 'L0_cond_ln_beta': _L0_cond_in['ln_beta'], 'L1_cond_ln_g': _L1_cond_in['ln_g'], 'L1_cond_ln_b': _L1_cond_in['ln_b'], 'L1_cond_subj_emb': _L1_cond_in['subj_emb'], 'L1_cond_hyp_w1': _L1_cond_in['hyp_w1'], 'L1_cond_hyp_b1': _L1_cond_in['hyp_b1'], 'L1_cond_hyp_w2': _L1_cond_in['hyp_w2'], 'L1_cond_hyp_b2': _L1_cond_in['hyp_b2'], 'L1_cond_sty_w1': _L1_cond_in['sty_w1'], 'L1_cond_sty_b1': _L1_cond_in['sty_b1'], 'L1_cond_sty_w2': _L1_cond_in['sty_w2'], 'L1_cond_sty_b2': _L1_cond_in['sty_b2'], 'L1_cond_router_w': _L1_cond_in['router_w'], 'L1_cond_exp_w1': _L1_cond_in['exp_w1'], 'L1_cond_exp_b1': _L1_cond_in['exp_b1'], 'L1_cond_exp_w2': _L1_cond_in['exp_w2'], 'L1_cond_exp_b2': _L1_cond_in['exp_b2']}

def reference(x, itok_B_0_15, itok_B_6_14, L0_cond_down_W, L0_cond_down_b, L0_cond_up_W, L0_cond_up_b, L0_cond_expert_W, L0_cond_expert_b, L0_cond_domain_emb, L0_cond_ln_gamma, L0_cond_ln_beta, L1_cond_ln_g, L1_cond_ln_b, L1_cond_subj_emb, L1_cond_hyp_w1, L1_cond_hyp_b1, L1_cond_hyp_w2, L1_cond_hyp_b2, L1_cond_sty_w1, L1_cond_sty_b1, L1_cond_sty_w2, L1_cond_sty_b2, L1_cond_router_w, L1_cond_exp_w1, L1_cond_exp_b1, L1_cond_exp_w2, L1_cond_exp_b2):
    import jax
    import jax.numpy as jnp

    def _L0_cond_ref(hidden_states, domain_id, down_W, down_b, up_W, up_b, expert_W, expert_b, domain_emb, ln_gamma, ln_beta):
        import jax, jax.numpy as jnp
        import numpy as np
        B, S, D = (32, 128, 128)
        A = 32
        E = 16
        LN_EPS = 1e-05
        residual = hidden_states
        hidden = jnp.einsum('bsd,ad->bsa', hidden_states, down_W) + down_b
        hidden = jax.nn.gelu(hidden, approximate=False)
        valid = (domain_id >= 0) & (domain_id < E)
        idx = jnp.clip(domain_id, 0, E - 1)
        Wsel = expert_W[idx]
        bsel = expert_b[idx]
        expert_out = jnp.einsum('bsa,boa->bso', hidden, Wsel) + bsel[:, None, :]
        domain_output = jnp.where(valid[:, None, None], expert_out, hidden)
        hidden = domain_output + domain_emb[idx][:, None, :]
        hidden = jnp.einsum('bsa,da->bsd', hidden, up_W) + up_b
        x = hidden + residual
        mu = jnp.mean(x, axis=-1, keepdims=True)
        var = jnp.mean(jnp.square(x - mu), axis=-1, keepdims=True)
        return (x - mu) * jax.lax.rsqrt(var + LN_EPS) * ln_gamma + ln_beta

    def _L1_cond_ref(x, subject_ids, ln_g, ln_b, subj_emb, hyp_w1, hyp_b1, hyp_w2, hyp_b2, sty_w1, sty_b1, sty_w2, sty_b2, router_w, exp_w1, exp_b1, exp_w2, exp_b2):
        import jax, jax.numpy as jnp
        import numpy as np
        D = 128
        E = 8
        FF = 512
        TOPK = 2
        S = 32
        SE = 64
        SH = 128
        B, T = (2, 256)

        def _forward(x, subject_ids, ln_g, ln_b, subj_emb, hyp_w1, hyp_b1, hyp_w2, hyp_b2, sty_w1, sty_b1, sty_w2, sty_b2, router_w, exp_w1, exp_b1, exp_w2, exp_b2):
            mu = x.mean(-1, keepdims=True)
            var = x.var(-1, keepdims=True)
            h = (x - mu) * jax.lax.rsqrt(var + 1e-05) * ln_g + ln_b
            m_t = h.mean(1, keepdims=True)
            v_t = h.var(1, keepdims=True)
            h_norm = (h - m_t) * jax.lax.rsqrt(v_t + 1e-08)
            se = subj_emb[subject_ids]
            hyp = jax.nn.relu(se @ hyp_w1 + hyp_b1) @ hyp_w2 + hyp_b2
            sty = jax.nn.relu(hyp @ sty_w1 + sty_b1) @ sty_w2 + sty_b2
            gamma, beta = jnp.split(sty, 2, axis=-1)
            gamma = jax.nn.softplus(gamma) + 1e-08
            h = h_norm * gamma[:, None, :] + beta[:, None, :]
            h_flat = h.reshape(-1, D)
            probs = jax.nn.softmax(h_flat @ router_w, axis=-1)
            gates, idx = jax.lax.top_k(probs, TOPK)
            gates = gates / gates.sum(-1, keepdims=True)
            N = h_flat.shape[0]
            combine = jnp.zeros((N, E), h_flat.dtype).at[jnp.arange(N)[:, None], idx].add(gates)
            hid = jax.nn.relu(jnp.einsum('nd,edf->nef', h_flat, exp_w1) + exp_b1)
            eout = jnp.einsum('nef,efd->ned', hid, exp_w2) + exp_b2
            y = jnp.einsum('ned,ne->nd', eout, combine)
            return x + y.reshape(x.shape)
        return _forward(x, subject_ids, ln_g, ln_b, subj_emb, hyp_w1, hyp_b1, hyp_w2, hyp_b2, sty_w1, sty_b1, sty_w2, sty_b2, router_w, exp_w1, exp_b1, exp_w2, exp_b2)
    x = _L0_cond_ref(x, itok_B_0_15, L0_cond_down_W, L0_cond_down_b, L0_cond_up_W, L0_cond_up_b, L0_cond_expert_W, L0_cond_expert_b, L0_cond_domain_emb, L0_cond_ln_gamma, L0_cond_ln_beta)
    x = _L1_cond_ref(x, itok_B_6_14, L1_cond_ln_g, L1_cond_ln_b, L1_cond_subj_emb, L1_cond_hyp_w1, L1_cond_hyp_b1, L1_cond_hyp_w2, L1_cond_hyp_b2, L1_cond_sty_w1, L1_cond_sty_b1, L1_cond_sty_w2, L1_cond_sty_b2, L1_cond_router_w, L1_cond_exp_w1, L1_cond_exp_b1, L1_cond_exp_w2, L1_cond_exp_b2)
    return x

_drawn_inputs = setup_inputs


def setup_inputs(seed=0):
    import zlib

    import numpy as np

    out = dict(_drawn_inputs(seed))
    spreads = {'L0_cond_ln_gamma': (1.0, 0.2),
     'L0_cond_ln_beta': (0.0, 0.1),
     'L1_cond_ln_g': (1.0, 0.2),
     'L1_cond_ln_b': (0.0, 0.1),
     'L1_cond_hyp_b1': (0.0, 0.1),
     'L1_cond_hyp_b2': (0.0, 0.1),
     'L1_cond_sty_b1': (0.0, 0.1),
     'L1_cond_sty_b2': (0.0, 0.1),
     'L1_cond_exp_b1': (0.0, 0.1),
     'L1_cond_exp_b2': (0.0, 0.1)}
    factors = {}
    for name, (base, spread) in spreads.items():
        noise = np.random.default_rng([zlib.crc32(name.encode()), seed]).standard_normal(out[name].shape)
        drawn = base * np.exp(spread * noise) if base else spread * noise
        out[name] = jnp.asarray(drawn.astype(out[name].dtype))
    for name, factor in factors.items():
        out[name] = (out[name] * factor).astype(out[name].dtype)
    return out
```

```python
from contextlib import ExitStack

import concourse.bass as bass
from concourse import mybir

F32 = mybir.dt.float32
F32R = mybir.dt.float32r
I32 = mybir.dt.int32
U32 = mybir.dt.uint32
ALU = mybir.AluOpType
ACT = mybir.ActivationFunctionType
AX_X = mybir.AxisListType.X

P = 128
B, S, D = 8, 256, 128
A, NDOM = 32, 16
NSUBJ, SE = 32, 64
E, FF = 8, 512
GB = 2
G = B // GB
N = GB * S
TI = N // P
FC = FF // P
CH = E * FC
HALF = 64
LEAD = 3
SPLIT_AT = 8
LN_EPS, T_EPS, SOFTPLUS_EPS = 1e-5, 1e-8, 1e-8

ROW_LN_G, ROW_LN_B, ROW_HYP_B1, ROW_HYP_B2 = 32, 33, 34, 35
ROW_GAMMA_B, ROW_BETA_B, ROW_STY_B1, ROW_DOWN_B = 36, 37, 38, 39
ROWS = 40

HI_ENGINE = ("act", "dve", "act", "pool")


def program(nc, x, dom, sub, down_W, down_b, up_W, up_b, expert_W, expert_b, domain_emb, ln_gamma,
            ln_beta, ln_g, ln_b, subj_emb, hyp_w1, hyp_b1, hyp_w2, hyp_b2, sty_w1, sty_b1, sty_w2,
            sty_b2, router_w, exp_w1, exp_b1, exp_w2, exp_b2, out):
    ctx = ExitStack()
    with ctx:
        def sb(name, shape, dt=F32):
            return ctx.enter_context(nc.sbuf_tensor(name, shape, dt))

        def bank(name):
            return ctx.enter_context(nc.psum_tensor(name, [P, 512], F32))

        def sem(name):
            return ctx.enter_context(nc.semaphore(name))

        dom_i = sb("dom_i", [P, B], I32)
        sub_i = sb("sub_i", [NSUBJ, B], I32)
        down_sb = sb("down_sb", [A, D])
        down_T = sb("down_T", [P, A])
        up_sb4 = sb("up_sb4", [P, 4, A])
        up_rep = sb("up_rep", [P, D])
        up_ext = sb("up_ext", [A + 1, D])
        ew_sb = sb("ew_sb", [P, 4, A])
        eb_sb = sb("eb_sb", [NDOM, A])
        demb_sb = sb("demb_sb", [NDOM, A])
        lng_bc = sb("lng_bc", [P, D])
        lnb_bc = sb("lnb_bc", [P, D])
        rows = sb("rows", [ROWS, P])
        cols = sb("cols", [P, ROWS])
        subj_sb = sb("subj_sb", [NSUBJ, SE])
        hw1_sb = sb("hw1_sb", [SE, P])
        hw2_sb = sb("hw2_sb", [P, P])
        sw1_sb = sb("sw1_sb", [P, HALF])
        sw2_sb = sb("sw2_sb", [HALF, 2 * D])
        rw_sb = sb("rw_sb", [P, E])
        b2_sb = sb("b2_sb", [2 * E, D])
        b2_hi = sb("b2_hi", [2 * E, D], F32R)
        b2_lo = sb("b2_lo", [2 * E, D], F32R)
        w1_sb = sb("w1_sb", [P, E, FF])
        w2_sb = sb("w2_sb", [P, E, FC, D])
        w1_hi = sb("w1_hi", [P, E, FF], F32R)
        w1_lo = sb("w1_lo", [P, E, FF], F32R)
        w2_hi = sb("w2_hi", [P, E, FC, D], F32R)
        w2_lo = sb("w2_lo", [P, E, FC, D], F32R)
        ident = sb("ident", [P, P])
        minus_half = sb("minus_half", [P, TI])
        iota_e = sb("iota_e", [P, E])
        pid = sb("pid", [NSUBJ, 1])
        row_i = sb("row_i", [P, 4], I32)
        eid_i = sb("eid_i", [P, 4], I32)
        eid = sb("eid", [P, 4])
        sel_f = sb("sel_f", [2 * E, E, P])
        sel = sb("sel", [2 * E, E, P], F32R)
        dom_f = sb("dom_f", [P, B])
        dom_c = sb("dom_c", [P, B])
        valid = sb("valid", [P, B])
        is_e = sb("is_e", [P, 4, B])
        m_e = sb("m_e", [P, 4, B])
        w_sel = sb("w_sel", [P, 4, B, HALF])
        rest = sb("rest", [A + 1, B, HALF])
        inval = sb("inval", [A, B])
        oh_d = sb("oh_d", [NDOM, B])
        oh_v = sb("oh_v", [NDOM, B])
        M2 = sb("M2", [P, G, GB * D])
        sub_f = sb("sub_f", [NSUBJ, B])
        sub_w = sb("sub_w", [NSUBJ, B])
        oh_s = sb("oh_s", [NSUBJ, B])
        se_sb = sb("se_sb", [SE, B])
        hyp_h = sb("hyp_h", [P, B])
        hyp_o = sb("hyp_o", [P, B])
        sty_h = sb("sty_h", [HALF, B])
        gz = sb("gz", [P, B])
        gabs = sb("gabs", [P, B])
        gexp = sb("gexp", [P, B])
        gln = sb("gln", [P, B])
        gamma = sb("gamma", [P, B])
        beta = sb("beta", [P, B])
        x_sb = sb("x_sb", [P, G, TI, D])
        xT = sb("xT", [P, G, N])
        hid = sb("hid", [P, G, S])
        hid_cur = sb("hid_cur", [P, S])
        x0 = sb("x0", [P, TI, D])
        st = sb("st", [P, TI, 6])
        mv = sb("mv", [P, TI, 2])
        ve = sb("ve", [P, TI])
        rstd = sb("rstd", [P, TI])
        xn = sb("xn", [P, TI, D])
        xg = sb("xg", [P, TI, D])
        x1 = x_sb
        hn = sb("hn", [P, TI, D])
        hf = sb("hf", [P, N])
        st_t = sb("st_t", [P, GB, 6])
        mv_t = sb("mv_t", [P, GB, 2])
        ve_t = sb("ve_t", [P, GB])
        rstd_t = sb("rstd_t", [P, GB])
        aff_s = sb("aff_s", [P, GB])
        aff_m = sb("aff_m", [P, GB])
        aff_b = sb("aff_b", [P, GB])
        h2 = sb("h2", [P, N])
        h2_hi = sb("h2_hi", [P, G, N], F32R)
        h2_lo = sb("h2_lo", [P, G, N], F32R)
        lmax = sb("lmax", [P, TI])
        lsh = sb("lsh", [P, TI, E])
        lex = sb("lex", [P, TI, E])
        lsum = sb("lsum", [P, TI])
        lrec = sb("lrec", [P, TI])
        prob = sb("prob", [P, TI, E])
        top = sb("top", [P, TI, 8])
        top_i = sb("top_i", [P, TI, 8], U32)
        top_f = sb("top_f", [P, TI, 2])
        gsum = sb("gsum", [P, TI])
        grec = sb("grec", [P, TI])
        gate = sb("gate", [P, TI, 2])
        oh0 = sb("oh0", [P, TI, E])
        oh1 = sb("oh1", [P, TI, E])
        c0 = sb("c0", [P, TI, E])
        c1 = sb("c1", [P, TI, E])
        comb = sb("comb", [P, TI, E])
        comb2 = sb("comb2", [P, TI, P])
        cT = sb("cT", [2 * E, N], F32R)
        r_sb = xT
        r_hi = sb("r_hi", [P, FC, N], F32R)
        r_lo = sb("r_lo", [P, FC, N], F32R)
        gate_bc = w_sel[:, 0:2, :, :].rearrange("p q b k -> p q (b k)")
        yg = sb("yg", [P, N])
        acc = sb("acc", [P, N])

        zb = [bank(f"zb{i}") for i in range(LEAD)]
        yb = [bank(f"yb{i}") for i in range(2)]
        bA = bank("bA")
        bB = bank("bB")
        bG = bank("bG")
        xT_ps = [zb[0], zb[1], zb[2], yb[0]]
        hid_ps = [yb[1][:, 0:S], bB[:, 0:S], zb[0][:, 0:S], zb[1][:, 0:S]]
        downT_ps, upT_ps = bA[:, 0:A], bA[:, 128:256]
        se_ps, hyp1_ps, hyp2_ps, sty1_ps = bA[0:SE, 0:B], bA[:, 0:B], bA[:, 0:B], bA[0:HALF, 0:B]
        gz_ps, bz_ps = bA[:, 0:B], bA[:, B:2 * B]
        cols_ps = bG[:, 0:ROWS]
        v_ps = zb[0][0:A, 0:B]
        M_ps = bG[:, :].rearrange("p (g d) -> p g d", g=G)

        ld_x = [sem(f"ld_x{g}") for g in range(G)]
        ld_ids, ld_adapt, ld_rows, ld_style, ld_ln, ld_b2 = (
            sem("ld_ids"), sem("ld_adapt"), sem("ld_rows"), sem("ld_style"), sem("ld_ln"), sem("ld_b2"))
        W_LOADS = [(0, 1), (1, 2), (2, 3), (3, 4), (4, 6), (6, 8)]
        ld_w = [sem(f"ld_w{i}") for i in range(len(W_LOADS))]
        ident_done = sem("ident_done")
        zeros_done = sem("zeros_done")
        iotas_done = sem("iotas_done")
        rows_clear = sem("rows_clear")
        pool_setup = sem("pool_setup")
        dve_setup = sem("dve_setup")
        act_setup = sem("act_setup")
        subj_onehot = sem("subj_onehot")
        sel_done = sem("sel_done")
        x_transposed = sem("x_transposed")
        xT_done_dve, xT_done_act = sem("xT_done_dve"), sem("xT_done_act")
        adapt_transposed, cols_transposed = sem("adapt_transposed"), sem("cols_transposed")
        downT_done, upT_done, cols_done = sem("downT_done"), sem("upT_done"), sem("cols_done")
        down_done = sem("down_done")
        hid_done = sem("hid_done")
        w_sel_done, oh_done, rest_done = sem("w_sel_done"), sem("oh_done"), sem("rest_done")
        v_done, M_done, M2_done = sem("v_done"), sem("M_done"), sem("M2_done")
        style_mm, style_ev = sem("style_mm"), sem("style_ev")
        gexp_done, gln_done, gamma_done = sem("gexp_done"), sem("gln_done"), sem("gamma_done")
        whi_done, wlo_done = sem("whi_done"), sem("wlo_done")
        wlo_pool_done = sem("wlo_pool_done")
        b2_done = sem("b2_done")
        hid_cur_done, up_done, x0_done = sem("hid_cur_done"), sem("up_done"), sem("x0_done")
        var1, rstd1, xn_done, x1_done = sem("var1"), sem("rstd1"), sem("xn_done"), sem("x1_done")
        var2, rstd2, hn_done, hnT_done = sem("var2"), sem("rstd2"), sem("hn_done"), sem("hnT_done")
        hf_done, var3, aff_done, h2_done = sem("hf_done"), sem("var3"), sem("aff_done"), sem("h2_done")
        h2hi_done, h2lo_done = sem("h2hi_done"), sem("h2lo_done")
        logits_done, lsh_done, lex_done, comb_done = (
            sem("logits_done"), sem("lsh_done"), sem("lex_done"), sem("comb_done"))
        combT_done, cT_done, b2t_done, acc_init = (
            sem("combT_done"), sem("cT_done"), sem("b2t_done"), sem("acc_init"))
        dve_front, pool_front = sem("dve_front"), sem("pool_front")
        z_done, r_done = sem("z_done"), sem("r_done")
        hi_done = {k: sem(f"hi_done_{k}") for k in ("act", "dve", "pool")}
        lo_done, l2_done = sem("lo_done"), sem("l2_done")
        gate_mm, gate_done, yg_done, acc_done = (
            sem("gate_mm"), sem("gate_done"), sem("yg_done"), sem("acc_done"))
        fin_done, out_done, stored = sem("fin_done"), sem("out_done"), sem("stored")

        def need(eng, s, value):
            if isinstance(value, int) and value <= 0:
                return
            eng.wait_ge(s, value)

        def need_apart(eng, s, value):
            if isinstance(value, int):
                need(eng, s, value)
                return
            value = eng.to_reg(value)
            eng.wait_ge(ident_done, 1)
            eng.wait_ge(s, value)

        def his(kind, f):
            return sum(k == kind for k in HI_ENGINE[:f])

        def chunk(t, s):
            return t + s // CH, (s % CH) // FC, s % FC

        def each_slot(step, t, first, last):
            for s in range(first, last):
                step(t, s)

        def whole(run, eng):
            each_slot(run, 0, 0, SPLIT_AT)
            with eng.Fori(0, G - 1) as t:
                each_slot(run, t, SPLIT_AT, CH)
                each_slot(run, t + 1, 0, SPLIT_AT)
            each_slot(run, G - 1, SPLIT_AT, CH)

        def in_loop(t):
            return not isinstance(t, int)

        block = ctx.enter_context(nc.Block())

        @block.sync
        def _(sp):
            x_v = x.rearrange("b s d -> (b s) d").rearrange("(g i p) d -> g p i d", g=G, p=P)

            def load_x(g):
                sp.dma_start(x_sb[:, g, :, :], x_v[g]).then_inc(ld_x[g], 16)

            def load_w(i):
                a, b = W_LOADS[i]
                sp.dma_start(w1_sb[:, a:b, :], exp_w1[a:b].rearrange("e d f -> d e f")).then_inc(ld_w[i], 16)
                sp.dma_start(w2_sb[:, a:b, :, :], exp_w2[a:b].rearrange("e (c p) d -> p e c d", p=P))\
                  .then_inc(ld_w[i], 16)

            load_x(0)
            load_x(1)
            load_w(0)
            load_x(2)
            load_x(3)
            for i in range(1, len(W_LOADS)):
                load_w(i)
            out_v = out.rearrange("b s d -> (b s) d").rearrange("(g i p) d -> p g i d", g=G, p=P)

            def store(t):
                need(sp, out_done, t + 1)
                sp.dma_start(out_v[:, bass.ds(t, 1)], x1[:, bass.ds(t, 1)]).then_inc(stored, 16)
            with sp.Fori(0, G - 1) as t:
                store(t)
            store(G - 1)
            sp.wait_ge(stored, 16 * G)

        @block.gpsimd
        def _(pool):
            gp = nc.gpsimd
            n_setup = [0]

            def link(ins):
                n_setup[0] += 1
                ins.then_inc(pool_setup, 1)
                pool.wait_ge(pool_setup, n_setup[0])

            link(gp.memset(ident[:, :], 0.0))
            gp.affine_select(out=ident[:, :], in_=ident[:, :], compare_op=ALU.not_equal, fill=1.0, base=0,
                             pattern=[[-1, P]], channel_multiplier=1).then_inc(ident_done, 1)
            gp.memset(rows[:, :], 0.0).then_inc(rows_clear, 1)
            pool.dma_start(subj_sb[:, :], subj_emb).then_inc(ld_style, 16)
            pool.dma_start(hw1_sb[:, :], hyp_w1).then_inc(ld_style, 16)
            pool.dma_start(hw2_sb[:, :], hyp_w2).then_inc(ld_style, 16)
            pool.dma_start(sw1_sb[:, :], sty_w1).then_inc(ld_style, 16)
            pool.dma_start(sw2_sb[:, :], sty_w2).then_inc(ld_style, 16)
            pool.dma_start(rw_sb[:, :], router_w).then_inc(ld_style, 16)
            pool.dma_start(lng_bc[:, :], ln_gamma.rearrange("(o d) -> o d", o=1).to_broadcast([P, D])).then_inc(ld_ln, 16)
            pool.dma_start(lnb_bc[:, :], ln_beta.rearrange("(o d) -> o d", o=1).to_broadcast([P, D])).then_inc(ld_ln, 16)
            gp.iota(row_i[:, :], [[P, 4]], base=0, channel_multiplier=1)
            gp.iota(pid[:, :], [[0, 1]], base=0, channel_multiplier=1, allow_small_or_imprecise_dtypes=True)
            gp.iota(iota_e[:, :], [[1, E]], base=0, channel_multiplier=0,
                    allow_small_or_imprecise_dtypes=True).then_inc(iotas_done, 1)
            gp.memset(w_sel[:, :, :, :], 0.0)
            gp.memset(rest[:, :, :], 0.0).then_inc(zeros_done, 1)
            gp.memset(hid[:, :, :], 0.0)
            gp.memset(M2[:, :, :], 0.0).then_inc(zeros_done, 1)
            pool.wait_ge(ld_ids, 32)
            link(gp.tensor_copy(sub_f[:, :], sub_i[:, :]))
            link(gp.tensor_scalar(sub_w[:, :], sub_f[:, :], 0.0, float(NSUBJ), ALU.is_lt, ALU.mult))
            link(gp.tensor_tensor(sub_w[:, :], sub_w[:, :], sub_f[:, :], ALU.add))
            link(gp.tensor_scalar(sub_w[:, :], sub_w[:, :], 0.0, float(NSUBJ - 1), ALU.max, ALU.min))
            gp.tensor_scalar(oh_s[:, :], sub_w[:, :], pid[:, :], None, ALU.is_equal).then_inc(subj_onehot, 1)
            gp.memset(minus_half[:, :], -0.5)
            link(gp.memset(sel_f[:, :, :], 0.0))
            for base in (0, -E):
                link(gp.affine_select(out=sel_f[:, :, :], in_=sel_f[:, :, :], compare_op=ALU.not_equal, fill=1.0,
                                      base=base, pattern=[[-1, E], [0, P]], channel_multiplier=1))
            gp.tensor_copy(sel[:, :, :], sel_f[:, :, :]).then_inc(sel_done, 1)
            gp.memset(comb2[:, :, :], 0.0).then_inc(zeros_done, 1)

            PF = 7

            class Front:
                def __init__(self, t):
                    self.base, self.n = 0, 0
                    if in_loop(t):
                        pool.sem_clear(pool_front)

            front = [None]

            def flink(ins):
                f = front[0]
                f.n += 1
                ins.then_inc(pool_front, 1)
                pool.wait_ge(pool_front, f.base + f.n)

            def hid_copy(T):
                if not in_loop(T):
                    pool.wait_ge(hid_done, GB * G)
                need_apart(pool, up_done, T)
                gp.tensor_copy(hid_cur[:, :], hid[:, bass.ds(T, 1), :] if in_loop(T) else hid[:, T, :])\
                  .then_inc(hid_cur_done, 1)

            def rstd_tokens(T, var, done):
                need_apart(pool, var, T + 1)
                flink(gp.tensor_scalar(ve[:, :], mv[:, :, 1], LN_EPS, None, ALU.add))
                gp.tensor_tensor(rstd[:, :], ve[:, :], minus_half[:, :], ALU.pow).then_inc(done, 1)

            def scale_x1(T):
                if not in_loop(T):
                    pool.wait_ge(ld_ln, 32)
                need(pool, xn_done, T + 1)
                flink(gp.tensor_tensor(xg[:, :, :], xn[:, :, :], lng_bc[:, None, :].to_broadcast([P, TI, D]), ALU.mult))
                dst = x1[:, bass.ds(T, 1), :, :].rearrange("p o i d -> p (o i) d") if in_loop(T) else x1[:, T, :, :]
                gp.tensor_tensor(dst, xg[:, :, :], lnb_bc[:, None, :].to_broadcast([P, TI, D]), ALU.add)\
                  .then_inc(x1_done, 1)

            def style_affine(T):
                need_apart(pool, var3, T + 1)
                if not in_loop(T):
                    pool.wait_ge(gamma_done, 2)
                gam = gamma[:, bass.ds(T * GB, GB)]
                bet = beta[:, bass.ds(T * GB, GB)]
                flink(gp.tensor_scalar(ve_t[:, :], mv_t[:, :, 1], T_EPS, None, ALU.add))
                flink(gp.tensor_tensor(rstd_t[:, :], ve_t[:, :], minus_half[:, 0:GB], ALU.pow))
                flink(gp.tensor_tensor(aff_s[:, :], rstd_t[:, :], gam, ALU.mult))
                flink(gp.tensor_tensor(aff_m[:, :], mv_t[:, :, 0], aff_s[:, :], ALU.mult))
                gp.tensor_tensor(aff_b[:, :], bet, aff_m[:, :], ALU.subtract).then_inc(aff_done, 1)

            def round_hi(t, s):
                T, e, f = chunk(t, s)
                if HI_ENGINE[f] != "pool":
                    return
                n = CH * T + s % CH
                need_apart(pool, l2_done, n - FC + 1)
                need_apart(pool, r_done, n + 1)
                gp.tensor_copy(r_hi[:, f, :], r_sb[:, f, :]).then_inc(hi_done["pool"], 1)

            def accumulate(t, u):
                if u < 0:
                    t, u = t - 1, u + E
                n = E * t + u
                if u == 0:
                    need(pool, acc_init, t + 1)
                need(pool, yg_done, n + 1)
                need(pool, acc_done, n)
                gp.tensor_tensor(acc[:, :], acc[:, :], yg[:, :], ALU.add).then_inc(acc_done, 1)

            def fronts(T, s):
                if s == 8:
                    hid_copy(T)
                if s == 12:
                    front[0] = Front(T)
                    rstd_tokens(T, var1, rstd1)
                if s == 14:
                    scale_x1(T)
                if s == 17:
                    rstd_tokens(T, var2, rstd2)
                if s == 22:
                    style_affine(T)

            def split_lo(e):
                i = next(i for i, (a, b) in enumerate(W_LOADS) if a <= e < b)
                pool.wait_ge(ld_w[i], 32)
                pool.wait_ge(whi_done, 2 * e + 2)
                gp.tensor_tensor(w2_lo[:, e], w2_sb[:, e], w2_hi[:, e].bitcast(F32), ALU.subtract)\
                  .then_inc(wlo_pool_done, 1)

            for s in range(SPLIT_AT, 17):
                fronts(0, s)
            rstd_tokens(0, var2, rstd2)
            split_lo(0)
            style_affine(0)
            split_lo(1)
            for s in range(LEAD):
                round_hi(0, s)

            def run(t, s):
                if not in_loop(t) and t == 0 and s < SPLIT_AT and s + 2 < E:
                    split_lo(s + 2)
                if in_loop(t) and s >= SPLIT_AT:
                    fronts(t + 1, s)
                if not (not in_loop(t) and t == G - 1 and s + LEAD >= CH):
                    round_hi(t, s + LEAD)
                if s % FC == 1 and not (not in_loop(t) and t == 0 and s < FC):
                    accumulate(t, s // FC - 1)
            whole(run, pool)
            accumulate(G - 1, E - 1)
            assert front[0].n == PF

        @block.scalar
        def _(act):
            sc = nc.scalar
            act.dma_start(dom_i[:, :], dom.rearrange("(o b) -> o b", o=1).to_broadcast([P, B])).then_inc(ld_ids, 16)
            act.dma_start(sub_i[:, :], sub.rearrange("(o b) -> o b", o=1).to_broadcast([NSUBJ, B])).then_inc(ld_ids, 16)
            act.dma_start(down_sb[:, :], down_W).then_inc(ld_adapt, 16)
            act.dma_start(up_sb4[:, :, :], up_W.rearrange("d (o a) -> d o a", o=1).to_broadcast([P, 4, A])).then_inc(ld_adapt, 16)
            act.dma_start(ew_sb[:, :, :], expert_W.rearrange("e o a -> (e o) a").rearrange("(t p) a -> p t a", p=P)).then_inc(ld_adapt, 16)
            act.dma_start(eb_sb[:, :], expert_b).then_inc(ld_adapt, 16)
            act.dma_start(demb_sb[:, :], domain_emb).then_inc(ld_adapt, 16)
            act.dma_start(up_ext[A:A + 1, :], up_b.rearrange("(o d) -> o d", o=1)).then_inc(ld_adapt, 16)
            act.wait_ge(rows_clear, 1)

            def row(r, vec, c0=0):
                n = vec.shape[0]
                act.dma_start(rows[r:r + 1, c0:c0 + n], vec.rearrange("(o n) -> o n", o=1)).then_inc(ld_rows, 16)
            row(ROW_DOWN_B, down_b)
            row(ROW_DOWN_B, down_b, HALF)
            act.dma_start(rows[0:CH, :], exp_b1.rearrange("e (c f) -> (e c) f", f=P)).then_inc(ld_rows, 16)
            act.dma_start(rows[ROW_GAMMA_B:ROW_BETA_B + 1, :], sty_b2.rearrange("(r n) -> r n", r=2)).then_inc(ld_rows, 16)
            for r, vec in ((ROW_LN_G, ln_g), (ROW_LN_B, ln_b), (ROW_HYP_B1, hyp_b1), (ROW_HYP_B2, hyp_b2),
                           (ROW_STY_B1, sty_b1)):
                row(r, vec)
            act.dma_start(b2_sb[0:E, :], exp_b2).then_inc(ld_b2, 16)
            act.dma_start(b2_sb[E:2 * E, :], exp_b2).then_inc(ld_b2, 16)

            def gelu(g):
                act.wait_ge(down_done, g + 1)
                for j in range(GB):
                    r = slice(HALF * j, HALF * j + A)
                    sc.activation(hid[r, g, :], hid_ps[g][r, :], ACT.Gelu,
                                  bias=cols[r, ROW_DOWN_B:ROW_DOWN_B + 1]).then_inc(hid_done, 1)
            act.wait_ge(cols_done, 1)
            act.wait_ge(zeros_done, 2)
            gelu(0)
            for g in (2, 3):
                act.wait_ge(x_transposed, g + 1)
                sc.activation(xT[:, g, :], xT_ps[g][:, :], ACT.Copy).then_inc(xT_done_act, 1)
                gelu(g - 1)
            gelu(3)
            act.wait_ge(style_ev, 5)
            sc.activation(gexp[:, :], gabs[:, :], ACT.Exp, scale=-1.0).then_inc(gexp_done, 1)
            act.wait_ge(gexp_done, 1)
            sc.activation(gln[:, :], gexp[:, :], ACT.Ln, bias=1.0).then_inc(gln_done, 1)

            def split_hi(e):
                i = next(i for i, (a, b) in enumerate(W_LOADS) if a <= e < b)
                act.wait_ge(ld_w[i], 32)
                sc.activation(w1_hi[:, e, :], w1_sb[:, e, :], ACT.Copy).then_inc(whi_done, 1)
                sc.activation(w2_hi[:, e], w2_sb[:, e], ACT.Copy).then_inc(whi_done, 1)

            def take_hf(T):
                need(act, hnT_done, T + 1)
                sc.activation(hf[:, :], bA[:, :], ACT.Identity, bias=cols[:, ROW_LN_B:ROW_LN_B + 1],
                              scale=cols[:, ROW_LN_G:ROW_LN_G + 1]).then_inc(hf_done, 1)

            def style(T):
                need(act, aff_done, T + 1)
                for j in range(GB):
                    sc.activation(h2[:, j * S:(j + 1) * S], hf[:, j * S:(j + 1) * S], ACT.Identity,
                                  bias=aff_b[:, j:j + 1], scale=aff_s[:, j:j + 1]).then_inc(h2_done, 1)

            def h2_round(T):
                need(act, h2_done, GB * (T + 1))
                dst = h2_hi[:, bass.ds(T, 1), :].rearrange("p o n -> p (o n)") if in_loop(T) else h2_hi[:, T, :]
                sc.activation(dst, h2[:, :], ACT.Copy).then_inc(h2hi_done, 1)

            def softmax_exp(T):
                need(act, lsh_done, T + 1)
                sc.activation(lex[:, :, :], lsh[:, :, :], ACT.Exp).then_inc(lex_done, 1)

            def take_cT(T):
                need(act, combT_done, T + 1)
                sc.activation(cT[:, :], bB[0:2 * E, :], ACT.Copy).then_inc(cT_done, 1)

            def init_acc(T):
                need(act, b2t_done, T + 1)
                need(act, fin_done, T)
                sc.activation(acc[:, :], bB[:, :], ACT.Copy).then_inc(acc_init, 1)

            def relu(t, s):
                T, e, f = chunk(t, s)
                n = CH * T + s % CH
                need(act, z_done, n + 1)
                need(act, lo_done, n - FC + 1)
                sc.activation(r_sb[:, f, :], zb[s % CH % LEAD][:, :], ACT.Relu,
                              bias=cols[:, e * FC + f:e * FC + f + 1]).then_inc(r_done, 1)
                if HI_ENGINE[f] == "act":
                    need(act, l2_done, n - FC + 1)
                    need(act, r_done, n + 1)
                    sc.activation(r_hi[:, f, :], r_sb[:, f, :], ACT.Copy).then_inc(hi_done["act"], 1)

            def take_gate(t, u):
                n = E * t + u
                need(act, gate_mm, n + 1)
                need(act, yg_done, n - 1)
                sc.activation(gate_bc[:, u % 2, :], bG[:, :], ACT.Copy).then_inc(gate_done, 1)

            split_hi(0)
            take_hf(0)
            split_hi(1)
            style(0)
            h2_round(0)
            for s in range(LEAD):
                relu(0, s)
            softmax_exp(0)
            take_cT(0)

            def run(t, s):
                prologue = not in_loop(t) and t == 0
                if prologue and s < SPLIT_AT and s + 2 < E:
                    split_hi(s + 2)
                if not (not in_loop(t) and t == G - 1 and s + LEAD >= CH):
                    relu(t, s + LEAD)
                if s % FC == 2:
                    take_gate(t, s // FC)
                if s == 4:
                    init_acc(t)
                if in_loop(t) and s >= SPLIT_AT:
                    if s == 20:
                        take_hf(t + 1)
                    if s == 23:
                        style(t + 1)
                    if s == 24:
                        h2_round(t + 1)
                    if s == 27:
                        softmax_exp(t + 1)
                    if s == 31:
                        take_cT(t + 1)
            whole(run, act)

        @block.vector
        def _(dve):
            v = nc.vector
            n_setup = [0]

            def link(ins):
                n_setup[0] += 1
                ins.then_inc(dve_setup, 1)
                dve.wait_ge(dve_setup, n_setup[0])

            def split_lo(e):
                i = next(i for i, (a, b) in enumerate(W_LOADS) if a <= e < b)
                dve.wait_ge(ld_w[i], 32)
                dve.wait_ge(whi_done, 2 * e + 1)
                v.tensor_tensor(w1_lo[:, e, :], w1_sb[:, e, :], w1_hi[:, e, :].bitcast(F32), ALU.subtract)\
                 .then_inc(wlo_done, 1)

            dve.wait_ge(ld_ids, 32)
            link(v.tensor_copy(dom_f[:, :], dom_i[:, :]))
            link(v.tensor_scalar(dom_c[:, :], dom_f[:, :], 0.0, float(NDOM - 1), ALU.max, ALU.min))
            dve.wait_ge(iotas_done, 1)
            link(v.tensor_scalar(eid_i[:, :], row_i[:, :], 5, None, ALU.arith_shift_right))
            link(v.tensor_copy(eid[:, :], eid_i[:, :]))
            link(v.tensor_tensor(valid[:, :], dom_f[:, :], dom_c[:, :], ALU.is_equal))
            link(v.tensor_tensor(is_e[:, :, :], dom_c[:, None, :].to_broadcast([P, 4, B]),
                                 eid[:, :, None].to_broadcast([P, 4, B]), ALU.is_equal))
            link(v.tensor_tensor(m_e[:, :, :], is_e[:, :, :], valid[:, None, :].to_broadcast([P, 4, B]), ALU.mult))
            dve.wait_ge(ld_adapt, 96)
            dve.wait_ge(zeros_done, 1)
            for q in range(4):
                last = v.tensor_tensor(w_sel[:, q, :, 0:A], ew_sb[:, q, None, :].to_broadcast([P, B, A]),
                                       m_e[:, q, :, None].to_broadcast([P, B, A]), ALU.mult)
            last.then_inc(w_sel_done, 1)
            v.tensor_scalar(oh_d[:, :], dom_c[0:NDOM, :], pid[0:NDOM, :], None, ALU.is_equal).then_inc(oh_done, 1)
            dve.wait_ge(oh_done, 1)
            v.tensor_tensor(oh_v[:, :], oh_d[:, :], valid[0:NDOM, :], ALU.mult).then_inc(oh_done, 1)
            link(v.tensor_scalar(inval[:, :], valid[0:A, :], -1.0, 1.0, ALU.mult, ALU.add))
            dve.wait_ge(ident_done, 1)
            v.tensor_tensor(rest[0:A, :, 0:A], ident[0:A, None, 0:A].to_broadcast([A, B, A]),
                            inval[:, :, None].to_broadcast([A, B, A]), ALU.mult)
            v.memset(rest[A:A + 1, :, A:A + 1], 1.0)
            dve.wait_ge(zeros_done, 2)
            v.memset(hid[A:A + 1, :, :], 1.0)
            v.memset(hid[HALF + A:HALF + A + 1, :, :], 1.0).then_inc(rest_done, 1)
            dve.wait_ge(adapt_transposed, 1)
            v.tensor_copy(down_T[:, :], downT_ps).then_inc(downT_done, 1)
            v.tensor_copy(up_rep[:, :], upT_ps)
            v.tensor_copy(up_ext[0:A, :], upT_ps[0:A, :]).then_inc(upT_done, 1)
            dve.wait_ge(x_transposed, 1)
            v.tensor_copy(xT[:, 0, :], xT_ps[0][:, :]).then_inc(xT_done_dve, 1)
            dve.wait_ge(cols_transposed, 1)
            v.tensor_copy(cols[:, :], cols_ps).then_inc(cols_done, 1)
            dve.wait_ge(x_transposed, 2)
            v.tensor_copy(xT[:, 1, :], xT_ps[1][:, :]).then_inc(xT_done_dve, 1)
            dve.wait_ge(v_done, 1)
            v.tensor_copy(rest[0:A, :, A], v_ps).then_inc(rest_done, 1)
            dve.wait_ge(style_mm, 1)
            v.tensor_copy(se_sb[:, :], se_ps).then_inc(style_ev, 1)
            dve.wait_ge(cols_done, 1)
            dve.wait_ge(M_done, 1)
            for j in range(GB):
                r = slice(HALF * j, HALF * (j + 1))
                v.tensor_copy(M2[r, :, j * D:(j + 1) * D], M_ps[r, :, :]).then_inc(M2_done, 1)
            dve.wait_ge(style_mm, 2)
            v.tensor_scalar(hyp_h[:, :], hyp1_ps, cols[:, ROW_HYP_B1:ROW_HYP_B1 + 1], 0.0, ALU.add, ALU.max)\
             .then_inc(style_ev, 1)
            dve.wait_ge(style_mm, 3)
            v.tensor_scalar(hyp_o[:, :], hyp2_ps, cols[:, ROW_HYP_B2:ROW_HYP_B2 + 1], None, ALU.add).then_inc(style_ev, 1)
            dve.wait_ge(style_mm, 4)
            v.tensor_scalar(sty_h[:, :], sty1_ps, cols[0:HALF, ROW_STY_B1:ROW_STY_B1 + 1], 0.0, ALU.add, ALU.max)\
             .then_inc(style_ev, 1)
            dve.wait_ge(style_mm, 5)
            link(v.tensor_scalar(gz[:, :], gz_ps, cols[:, ROW_GAMMA_B:ROW_GAMMA_B + 1], None, ALU.add))
            v.scalar_tensor_tensor(gabs[:, :], gz[:, :], -1.0, gz[:, :], ALU.mult, ALU.max).then_inc(style_ev, 1)
            v.tensor_scalar(beta[:, :], bz_ps, cols[:, ROW_BETA_B:ROW_BETA_B + 1], None, ALU.add).then_inc(gamma_done, 1)

            DF = 15
            front = [0, 0]

            def begin(T):
                front[0], front[1] = 0, 0
                if in_loop(T):
                    dve.sem_clear(dve_front)

            def flink(ins, by_itself=False):
                front[1] += 1
                ins.then_inc(dve_front, 1)
                (need)(dve, dve_front, front[0] + front[1])

            def add_residual(T):
                need(dve, up_done, T + 1)
                src = x_sb[:, bass.ds(T, 1), :, :].rearrange("p o (c h) d -> p (o c) h d", c=GB) if in_loop(T) \
                    else x_sb[:, T, :, :].rearrange("p (c h) d -> p c h d", c=GB)
                v.tensor_tensor(x0[:, :, :].rearrange("p (c h) d -> p c h d", c=GB),
                                bA[:, :].rearrange("p (h c d) -> p c h d", h=S // P, c=GB), src,
                                ALU.add).then_inc(x0_done, 1)

            def stats(T, src, done, guard, value):
                need_apart(dve, guard, value)
                for i in range(TI):
                    last = v.bn_stats(st[:, i, :], src(i))
                flink(last, True)
                for i in range(TI):
                    last = v.bn_aggr(mv[:, i, :], st[:, i, :])
                last.then_inc(done, 1)

            def normalise(T, src, dst, ready, done):
                need_apart(dve, ready, T + 1)
                for i in range(TI):
                    last = v.tensor_scalar(dst[:, i, :], src(i), mv[:, i, 0:1], rstd[:, i:i + 1],
                                           ALU.subtract, ALU.mult)
                last.then_inc(done, 1)

            def x0_tile(i):
                return x0[:, i, :]

            def x1_tile(T):
                def tile(i):
                    return x1[:, bass.ds(T, 1), i, :].rearrange("p o d -> p (o d)") if in_loop(T) else x1[:, T, i, :]
                return tile

            def stats_over_time(T):
                need_apart(dve, hf_done, T + 1)
                for j in range(GB):
                    last = v.bn_stats(st_t[:, j, :], hf[:, j * S:(j + 1) * S])
                flink(last, True)
                for j in range(GB):
                    last = v.bn_aggr(mv_t[:, j, :], st_t[:, j, :])
                last.then_inc(var3, 1)

            def h2_rest(T):
                need(dve, h2hi_done, T + 1)
                if in_loop(T):
                    hi = h2_hi[:, bass.ds(T, 1), :].rearrange("p o n -> p (o n)")
                    lo = h2_lo[:, bass.ds(T, 1), :].rearrange("p o n -> p (o n)")
                else:
                    hi, lo = h2_hi[:, T, :], h2_lo[:, T, :]
                v.tensor_tensor(lo, h2[:, :], hi.bitcast(F32), ALU.subtract).then_inc(h2lo_done, 1)

            def softmax_shift(T):
                need(dve, logits_done, T + 1)
                lg = bB[:, 0:TI * E].rearrange("p (i e) -> p i e", i=TI)
                flink(v.tensor_reduce(lmax[:, :], lg, AX_X, ALU.max))
                v.tensor_tensor(lsh[:, :, :], lg, lmax[:, :, None].to_broadcast([P, TI, E]), ALU.subtract)\
                 .then_inc(lsh_done, 1)

            def router(T):
                need(dve, lex_done, T + 1)
                flink(v.tensor_reduce(lsum[:, :], lex[:, :, :], AX_X, ALU.add))
                flink(v.reciprocal(lrec[:, :], lsum[:, :]))
                flink(v.tensor_tensor(prob[:, :, :], lex[:, :, :], lrec[:, :, None].to_broadcast([P, TI, E]), ALU.mult), True)
                for i in range(TI):
                    last = v.max(top[:, i, :], prob[:, i, :])
                flink(last, True)
                for i in range(TI):
                    last = v.max_index(top_i[:, i, :], top[:, i, :], prob[:, i, :])
                flink(last)
                v.tensor_copy(top_f[:, :, :], top_i[:, :, 0:2])
                flink(v.tensor_tensor(gsum[:, :], top[:, :, 0], top[:, :, 1], ALU.add))
                flink(v.reciprocal(grec[:, :], gsum[:, :]))
                v.tensor_tensor(oh0[:, :, :], iota_e[:, None, :].to_broadcast([P, TI, E]),
                                top_f[:, :, 0:1].to_broadcast([P, TI, E]), ALU.is_equal)
                v.tensor_tensor(oh1[:, :, :], iota_e[:, None, :].to_broadcast([P, TI, E]),
                                top_f[:, :, 1:2].to_broadcast([P, TI, E]), ALU.is_equal)
                flink(v.tensor_tensor(gate[:, :, :], top[:, :, 0:2], grec[:, :, None].to_broadcast([P, TI, 2]), ALU.mult))
                v.tensor_tensor(c0[:, :, :], oh0[:, :, :], gate[:, :, 0:1].to_broadcast([P, TI, E]), ALU.mult)
                flink(v.tensor_tensor(c1[:, :, :], oh1[:, :, :], gate[:, :, 1:2].to_broadcast([P, TI, E]), ALU.mult))
                flink(v.tensor_tensor(comb[:, :, :], c0[:, :, :], c1[:, :, :], ALU.add))
                if not in_loop(T):
                    dve.wait_ge(zeros_done, 3)
                flink(v.tensor_copy(comb2[:, :, 0:E].bitcast(F32R), comb[:, :, :]))
                v.tensor_tensor(comb2[:, :, E:2 * E], comb[:, :, :], comb2[:, :, 0:E], ALU.subtract)\
                 .then_inc(comb_done, 1)

            def round_hi(t, s):
                T, e, f = chunk(t, s)
                if HI_ENGINE[f] != "dve":
                    return
                n = CH * T + s % CH
                need(dve, r_done, n + 1)
                need(dve, l2_done, n - FC + 1)
                v.tensor_copy(r_hi[:, f, :], r_sb[:, f, :]).then_inc(hi_done["dve"], 1)

            def take_lo(t, s):
                T, e, f = chunk(t, s)
                n = CH * T + s % CH
                kind = HI_ENGINE[f]
                need(dve, hi_done[kind], (E * T + e) * his(kind, FC) + his(kind, f + 1))
                need(dve, l2_done, n - FC + 1)
                v.tensor_tensor(r_lo[:, f, :], r_sb[:, f, :], r_hi[:, f, :].bitcast(F32), ALU.subtract)\
                 .then_inc(lo_done, 1)

            def apply_gate(t, u):
                if u < 0:
                    t, u = t - 1, u + E
                n = E * t + u
                need(dve, l2_done, FC * (n + 1))
                need(dve, gate_done, n + 1)
                need(dve, acc_done, n)
                v.tensor_tensor(yg[:, :], yb[u % 2][:, :], gate_bc[:, u % 2, :], ALU.mult).then_inc(yg_done, 1)

            def finish(t):
                need(dve, fin_done, t + 1)
                res = x1[:, bass.ds(t, 1), :, :].rearrange("p o i d -> p (o i) d") if in_loop(t) else x1[:, t, :, :]
                v.tensor_tensor(res, bA[:, :].rearrange("p (i d) -> p i d", i=TI), res, ALU.add)\
                 .then_inc(out_done, 1)

            begin(0)
            add_residual(0)
            stats(0, x0_tile, var1, x0_done, 1)
            normalise(0, x0_tile, xn, rstd1, xn_done)
            dve.wait_ge(gln_done, 1)
            link(v.scalar_tensor_tensor(gamma[:, :], gz[:, :], 0.0, gln[:, :], ALU.max, ALU.add))
            v.tensor_scalar(gamma[:, :], gamma[:, :], SOFTPLUS_EPS, None, ALU.add).then_inc(gamma_done, 1)
            dve.wait_ge(ld_b2, 32)
            link(v.tensor_copy(b2_hi[:, :], b2_sb[:, :]))
            v.tensor_tensor(b2_lo[:, :], b2_sb[:, :], b2_hi[:, :].bitcast(F32), ALU.subtract).then_inc(b2_done, 1)
            stats(0, x1_tile(0), var2, x1_done, 1)
            normalise(0, x1_tile(0), hn, rstd2, hn_done)
            split_lo(0)
            stats_over_time(0)
            split_lo(1)
            h2_rest(0)
            softmax_shift(0)
            for s in range(LEAD):
                round_hi(0, s)
                take_lo(0, s)
            router(0)

            def run(t, s):
                if not in_loop(t) and t == 0 and s < SPLIT_AT and s + 2 < E:
                    split_lo(s + 2)
                if not (not in_loop(t) and t == G - 1 and s + LEAD >= CH):
                    round_hi(t, s + LEAD)
                    take_lo(t, s + LEAD)
                if s % FC == 0 and not (not in_loop(t) and t == 0 and s == 0):
                    apply_gate(t, s // FC - 1)
                if s == 4 and not (not in_loop(t) and t == 0):
                    finish(t - 1)
                if in_loop(t) and s >= SPLIT_AT:
                    T = t + 1
                    if s == 10:
                        begin(T)
                        add_residual(T)
                    if s == 11:
                        stats(T, x0_tile, var1, x0_done, T + 1)
                    if s == 13:
                        normalise(T, x0_tile, xn, rstd1, xn_done)
                    if s == 16:
                        stats(T, x1_tile(T), var2, x1_done, T + 1)
                    if s == 18:
                        normalise(T, x1_tile(T), hn, rstd2, hn_done)
                    if s == 21:
                        stats_over_time(T)
                    if s == 25:
                        h2_rest(T)
                    if s == 26:
                        softmax_shift(T)
                    if s == 28:
                        router(T)
            assert front[1] == DF, front[1]
            whole(run, dve)
            apply_gate(G - 1, E - 1)
            finish(G - 1)

        @block.tensor
        def _(pe):
            te = nc.tensor

            def transpose_x(g):
                pe.wait_ge(ld_x[g], 16)
                for i in range(TI):
                    last = te.transpose(xT_ps[g][:, i * P:(i + 1) * P], x_sb[:, g, i, :], ident[:, :])
                last.then_inc(x_transposed, 1)

            def down(g):
                if g < 2:
                    pe.wait_ge(xT_done_dve, g + 1)
                else:
                    pe.wait_ge(xT_done_act, g - 1)
                for j in range(GB):
                    last = te.matmul(hid_ps[g][HALF * j:HALF * j + A, :], down_T[:, :], xT[:, g, j * S:(j + 1) * S],
                                     start=True, stop=True)
                last.then_inc(down_done, 1)

            pe.wait_ge(ident_done, 1)
            pe.wait_ge(ld_adapt, 96)
            te.transpose(downT_ps, down_sb[:, :], ident[0:A, 0:A])
            te.transpose(upT_ps, up_sb4[:, :, :].rearrange("p r a -> p (r a)"), ident[:, :]).then_inc(adapt_transposed, 1)
            transpose_x(0)
            pe.wait_ge(ld_rows, 16 * 9)
            te.transpose(cols_ps, rows[:, :], ident[0:ROWS, 0:ROWS]).then_inc(cols_transposed, 1)
            pe.wait_ge(downT_done, 1)
            down(0)
            transpose_x(1)
            pe.wait_ge(xT_done_dve, 1)
            pe.wait_ge(oh_done, 2)
            te.matmul(v_ps, eb_sb[:, :], oh_v[:, :], start=True, stop=False)
            te.matmul(v_ps, demb_sb[:, :], oh_d[:, :], start=False, stop=True).then_inc(v_done, 1)
            pe.wait_ge(upT_done, 1)
            pe.wait_ge(subj_onehot, 1)
            pe.wait_ge(ld_style, 96)
            te.matmul(se_ps, subj_sb[:, :], oh_s[:, :], start=True, stop=True).then_inc(style_mm, 1)
            down(1)
            transpose_x(2)
            pe.wait_ge(w_sel_done, 1)
            pe.wait_ge(cols_done, 1)
            pe.wait_ge(rest_done, 2)
            for g in range(G):
                seqs = slice(g * GB, (g + 1) * GB)
                for q in range(4):
                    te.matmul(M_ps[:, g, :], w_sel[:, q, seqs, :].rearrange("p c k -> p (c k)"), up_rep[:, :],
                              start=(q == 0), stop=False)
                last = te.matmul(M_ps[:, g, :], rest[:, seqs, :].rearrange("p c k -> p (c k)"), up_ext[:, :],
                                 start=False, stop=True)
            last.then_inc(M_done, 1)
            pe.wait_ge(style_ev, 1)
            te.matmul(hyp1_ps, hw1_sb[:, :], se_sb[:, :], start=True, stop=True).then_inc(style_mm, 1)
            down(2)
            transpose_x(3)
            pe.wait_ge(style_ev, 2)
            te.matmul(hyp2_ps, hw2_sb[:, :], hyp_h[:, :], start=True, stop=True).then_inc(style_mm, 1)
            down(3)
            pe.wait_ge(style_ev, 3)
            te.matmul(sty1_ps, sw1_sb[:, :], hyp_o[:, :], start=True, stop=True).then_inc(style_mm, 1)
            pe.wait_ge(style_ev, 4)
            te.matmul(gz_ps, sw2_sb[:, 0:D], sty_h[:, :], start=True, stop=True)
            te.matmul(bz_ps, sw2_sb[:, D:2 * D], sty_h[:, :], start=True, stop=True).then_inc(style_mm, 1)

            def up(T):
                need(pe, hid_cur_done, T + 1)
                if not (isinstance(T, int) and T == 0):
                    need(pe, yg_done, E * (T - 1) + 2)
                rhs = M2[:, bass.ds(T, 1), :].rearrange("p o n -> p (o n)") if in_loop(T) else M2[:, T, :]
                for h in range(S // P):
                    last = te.matmul(bA[:, h * GB * D:(h + 1) * GB * D], hid_cur[:, h * P:(h + 1) * P], rhs,
                                     start=True, stop=True)
                last.then_inc(up_done, 1)

            def transpose_hn(T):
                need(pe, hn_done, T + 1)
                for i in range(TI):
                    last = te.transpose(bA[:, i * P:(i + 1) * P], hn[:, i, :], ident[:, :])
                last.then_inc(hnT_done, 1)

            def logits(T):
                need(pe, h2_done, GB * (T + 1))
                need(pe, acc_init, T)
                for i in range(TI):
                    last = te.matmul(bB[:, i * E:(i + 1) * E], h2[:, i * P:(i + 1) * P], rw_sb[:, :],
                                     start=True, stop=True)
                last.then_inc(logits_done, 1)

            def transpose_comb(T):
                need(pe, comb_done, T + 1)
                for i in range(TI):
                    last = te.transpose(bB[:, i * P:(i + 1) * P], comb2[:, i, :], ident[:, :])
                last.then_inc(combT_done, 1)

            def bias2(T):
                need(pe, cT_done, T + 1)
                te.matmul(bB[:, :], b2_hi[:, :], cT[:, :], start=True, stop=False)
                te.matmul(bB[:, :], b2_lo[:, :], cT[:, :], start=False, stop=True).then_inc(b2t_done, 1)

            def gate_rows(t, u):
                need(pe, cT_done, t + 1)
                need(pe, gate_done, E * t + u)
                te.matmul(bG[:, :], sel[:, u, :], cT[:, :], start=True, stop=True).then_inc(gate_mm, 1)

            def finish(t):
                need(pe, acc_done, E * (t + 1))
                need(pe, hf_done, t + 2 if not (isinstance(t, int) and t == G - 1) else t + 1)
                for i in range(TI):
                    last = te.transpose(bA[:, i * P:(i + 1) * P], acc[:, i * P:(i + 1) * P], ident[:, :])
                last.then_inc(fin_done, 1)

            def tokens(buf, T):
                return buf[:, bass.ds(T, 1), :].rearrange("p o n -> p (o n)") if in_loop(T) else buf[:, T, :]

            def product1(t, s):
                T, e, f = chunk(t, s)
                n = CH * T + s % CH
                need(pe, r_done, n - (2 if s % CH < 2 else LEAD) + 1)
                z = zb[s % CH % LEAD]
                w = slice(f * P, (f + 1) * P)
                te.matmul(z[:, :], w1_lo[:, e, w], tokens(h2_hi, T), start=True, stop=False)
                te.matmul(z[:, :], w1_hi[:, e, w], tokens(h2_lo, T), start=False, stop=False)
                te.matmul(z[:, :], w1_hi[:, e, w], tokens(h2_hi, T), start=False, stop=True).then_inc(z_done, 1)

            def product2(t, s):
                e, f = s // FC, s % FC
                n = CH * t + s
                need(pe, lo_done, n + 1)
                if f == 0:
                    need(pe, yg_done, E * t + e - 1)
                y = yb[e % 2]
                te.matmul(y[:, :], w2_lo[:, e, f, :], r_hi[:, f, :], start=(f == 0), stop=False)
                te.matmul(y[:, :], w2_hi[:, e, f, :], r_lo[:, f, :], start=False, stop=False)
                te.matmul(y[:, :], w2_hi[:, e, f, :], r_hi[:, f, :], start=False, stop=(f == FC - 1)).then_inc(l2_done, 1)

            pe.wait_ge(M2_done, 2)
            pe.wait_ge(gamma_done, 1)
            up(0)
            transpose_hn(0)
            pe.wait_ge(hid_done, 2 * G)
            logits(0)
            pe.wait_ge(h2lo_done, 1)
            pe.wait_ge(wlo_done, 1)
            for s in range(LEAD):
                product1(0, s)
            transpose_comb(0)
            pe.wait_ge(b2_done, 1)
            pe.wait_ge(sel_done, 1)

            def run(t, s):
                prologue = not in_loop(t) and t == 0 and s < SPLIT_AT
                if not (not in_loop(t) and t == G - 1 and s + LEAD >= CH):
                    if s + LEAD == CH:
                        need(pe, h2lo_done, t + 2)
                    if not in_loop(t) and t == 0 and (s + LEAD) % FC == 0:
                        pe.wait_ge(wlo_done, (s + LEAD) // FC + 1)
                    product1(t, s + LEAD)
                if not in_loop(t) and t == 0 and s % FC == 0:
                    pe.wait_ge(wlo_pool_done, s // FC + 1)
                product2(t, s)
                if s == 1:
                    bias2(t)
                if s % FC == 1:
                    gate_rows(t, s // FC)
                if s == 3 and not (not in_loop(t) and t == 0):
                    finish(t - 1)
                if s == SPLIT_AT - 1 and not in_loop(t) and t == 0:
                    pe.wait_ge(wlo_done, E)
                    pe.wait_ge(wlo_pool_done, E)
                if in_loop(t) and s >= SPLIT_AT:
                    if s == 9:
                        up(t + 1)
                    if s == 19:
                        transpose_hn(t + 1)
                    if s == 25:
                        logits(t + 1)
                    if s == 30:
                        transpose_comb(t + 1)
            whole(run, pe)
            finish(G - 1)


_INS = ["x", "itok_B_0_15", "itok_B_6_14", "L0_cond_down_W", "L0_cond_down_b", "L0_cond_up_W", "L0_cond_up_b",
        "L0_cond_expert_W", "L0_cond_expert_b", "L0_cond_domain_emb", "L0_cond_ln_gamma", "L0_cond_ln_beta",
        "L1_cond_ln_g", "L1_cond_ln_b", "L1_cond_subj_emb", "L1_cond_hyp_w1", "L1_cond_hyp_b1",
        "L1_cond_hyp_w2", "L1_cond_hyp_b2", "L1_cond_sty_w1", "L1_cond_sty_b1", "L1_cond_sty_w2",
        "L1_cond_sty_b2", "L1_cond_router_w", "L1_cond_exp_w1", "L1_cond_exp_b1", "L1_cond_exp_w2",
        "L1_cond_exp_b2"]


def kernel(**inputs):
    import numpy as np
    import concourse.bacc as bacc
    from concourse.bass_utils import run_bass_kernel_spmd

    nc = bacc.Bacc("TRN2", target_bir_lowering=False, num_devices=1)
    arrays, args = {}, []
    for name in _INS:
        a = np.ascontiguousarray(inputs[name])
        arrays[f"in_{name}"] = a
        args.append(nc.dram_tensor(f"in_{name}", a.shape, mybir.dt.from_np(a.dtype), kind="ExternalInput").ap())
    args.append(nc.dram_tensor("result", (B, S, D), F32, kind="ExternalOutput").ap())
    program(nc, *args)
    return run_bass_kernel_spmd(nc, [arrays], core_ids=[0]).results[0]["result"]
```

```python
from contextlib import ExitStack

import concourse.bass as bass
from concourse import mybir

F32 = mybir.dt.float32
F32R = mybir.dt.float32r
I32 = mybir.dt.int32
U32 = mybir.dt.uint32
ALU = mybir.AluOpType
ACT = mybir.ActivationFunctionType
AX_X = mybir.AxisListType.X

P = 128
B, S, D = 8, 256, 128
A, NDOM = 32, 16
NSUBJ, SE = 32, 64
E, FF = 8, 512
GB = 2
G = B // GB
N = GB * S
TI = N // P
FC = FF // P
CH = E * FC
HALF = 64
LEAD = 3
SPLIT_AT = 6
LN_EPS, T_EPS, SOFTPLUS_EPS = 1e-5, 1e-8, 1e-8

COL_LN_G, COL_LN_B, COL_HYP_B1, COL_HYP_B2 = 32, 33, 34, 35
COL_GAMMA_B, COL_BETA_B, COL_STY_B1, COL_DOWN_B = 36, 37, 38, 39
COLS = 40


def packing(parts):
    at, n = {}, 0
    for name, width in parts:
        at[name] = (n, n + width)
        n += width
    return at, n


ADAPT, ADAPT_N = packing([("down_T", A), ("up_rep", D), ("up_ext", D), ("experts", 4 * A), ("expert_b", A),
                          ("domain_emb", A), ("cols", COLS), ("ident", P), ("eid", 4), ("pid", 1), ("iota_e", E)])
STYLE, STYLE_N = packing([("subj", SE), ("hyp_w1", P), ("hyp_w2", P), ("sty_w1", HALF), ("sty_w2", 2 * D),
                          ("router_w", E), ("ln_gamma", D), ("ln_beta", D)])
ROUTE, ROUTE_N = packing([("exp_b2", D), ("sel", E * P)])

HI_ENGINE = ("act", "dve", "act", "dve")


def program(nc, x, x_t, ids, adapt, style, route, w1, w2, out):
    ctx = ExitStack()
    with ctx:
        def sb(name, shape, dt=F32):
            return ctx.enter_context(nc.sbuf_tensor(name, shape, dt))

        def bank(name):
            return ctx.enter_context(nc.psum_tensor(name, [P, 512], F32))

        def sem(name):
            return ctx.enter_context(nc.semaphore(name))

        ids_sb = sb("ids_sb", [P, 2 * B], I32)
        adapt_sb = sb("adapt_sb", [P, ADAPT_N])
        style_sb = sb("style_sb", [P, STYLE_N])
        route_sb = sb("route_sb", [2 * E, ROUTE_N])

        def part(tile, at, name, rows=P):
            return tile[0:rows, at[name][0]:at[name][1]]

        down_T = part(adapt_sb, ADAPT, "down_T")
        up_rep = part(adapt_sb, ADAPT, "up_rep")
        up_ext = part(adapt_sb, ADAPT, "up_ext", A + 1)
        ew_sb = part(adapt_sb, ADAPT, "experts").rearrange("p (t a) -> p t a", t=4)
        eb_sb = part(adapt_sb, ADAPT, "expert_b", NDOM)
        demb_sb = part(adapt_sb, ADAPT, "domain_emb", NDOM)
        cols = part(adapt_sb, ADAPT, "cols")
        ident = part(adapt_sb, ADAPT, "ident")
        eid = part(adapt_sb, ADAPT, "eid")
        pid = part(adapt_sb, ADAPT, "pid", NSUBJ)
        iota_e = part(adapt_sb, ADAPT, "iota_e")
        subj_sb = part(style_sb, STYLE, "subj", NSUBJ)
        hw1_sb = part(style_sb, STYLE, "hyp_w1", SE)
        hw2_sb = part(style_sb, STYLE, "hyp_w2")
        sw1_sb = part(style_sb, STYLE, "sty_w1")
        sw2_sb = part(style_sb, STYLE, "sty_w2", HALF)
        rw_sb = part(style_sb, STYLE, "router_w")
        lng_bc = part(style_sb, STYLE, "ln_gamma")
        lnb_bc = part(style_sb, STYLE, "ln_beta")
        b2_sb = part(route_sb, ROUTE, "exp_b2", 2 * E)
        sel_f = part(route_sb, ROUTE, "sel", 2 * E)
        b2_hi = sb("b2_hi", [2 * E, D], F32R)
        b2_lo = sb("b2_lo", [2 * E, D], F32R)
        sel = sb("sel", [2 * E, E, P], F32R)
        w1_sb = sb("w1_sb", [P, E, FF])
        w2_sb = sb("w2_sb", [P, E, FC, D])
        w1_hi = sb("w1_hi", [P, E, FF], F32R)
        w1_lo = sb("w1_lo", [P, E, FF], F32R)
        w2_hi = sb("w2_hi", [P, E, FC, D], F32R)
        w2_lo = sb("w2_lo", [P, E, FC, D], F32R)
        minus_half = sb("minus_half", [P, TI])
        dom_f = sb("dom_f", [P, B])
        dom_c = sb("dom_c", [P, B])
        valid = sb("valid", [P, B])
        is_e = sb("is_e", [P, 4, B])
        m_e = sb("m_e", [P, 4, B])
        w_sel = sb("w_sel", [P, 4, B, HALF])
        rest = sb("rest", [A + 1, B, HALF])
        inval = sb("inval", [A, B])
        oh_d = sb("oh_d", [NDOM, B])
        oh_v = sb("oh_v", [NDOM, B])
        M2 = sb("M2", [P, G, GB * D])
        sub_f = sb("sub_f", [NSUBJ, B])
        sub_w = sb("sub_w", [NSUBJ, B])
        oh_s = sb("oh_s", [NSUBJ, B])
        se_sb = sb("se_sb", [SE, B])
        hyp_h = sb("hyp_h", [P, B])
        hyp_o = sb("hyp_o", [P, B])
        sty_h = sb("sty_h", [HALF, B])
        gz = sb("gz", [P, B])
        gabs = sb("gabs", [P, B])
        gexp = sb("gexp", [P, B])
        gln = sb("gln", [P, B])
        gamma = sb("gamma", [P, B])
        beta = sb("beta", [P, B])
        x_sb = sb("x_sb", [P, G, TI, D])
        xT = sb("xT", [P, G, N])
        hid = sb("hid", [P, G, S])
        hid_cur = sb("hid_cur", [P, S])
        x0 = sb("x0", [P, TI, D])
        st = sb("st", [P, TI, 6])
        mv = sb("mv", [P, TI, 2])
        ve = sb("ve", [P, TI])
        rstd = sb("rstd", [P, TI])
        xg = sb("xg", [P, TI, D])
        x1 = x_sb
        hn = sb("hn", [P, TI, D])
        ln_g2 = sb("ln_g2", [P, 1])
        mean_t = sb("mean_t", [P, GB])
        shift_t = sb("shift_t", [P, GB])
        gain_t = sb("gain_t", [P, GB])
        gb_t = sb("gb_t", [P, GB])
        st_t = sb("st_t", [P, GB, 6])
        mv_t = sb("mv_t", [P, GB, 2])
        ve_t = sb("ve_t", [P, GB])
        rstd_t = sb("rstd_t", [P, GB])
        aff_s = sb("aff_s", [P, GB])
        aff_b = sb("aff_b", [P, GB])
        h2 = sb("h2", [P, N])
        h2_hi = sb("h2_hi", [P, G, N], F32R)
        h2_lo = sb("h2_lo", [P, G, N], F32R)
        lmax = sb("lmax", [P, TI])
        lsh = sb("lsh", [P, TI, E])
        lex = sb("lex", [P, TI, E])
        lsum = sb("lsum", [P, TI])
        lrec = sb("lrec", [P, TI])
        prob = sb("prob", [P, TI, E])
        top = sb("top", [P, TI, 8])
        top_i = sb("top_i", [P, TI, 8], U32)
        top_f = sb("top_f", [P, TI, 2])
        gsum = sb("gsum", [P, TI])
        grec = sb("grec", [P, TI])
        gate = sb("gate", [P, TI, 2])
        oh0 = sb("oh0", [P, TI, E])
        oh1 = sb("oh1", [P, TI, E])
        c0 = sb("c0", [P, TI, E])
        c1 = sb("c1", [P, TI, E])
        comb = sb("comb", [P, TI, E])
        comb2 = sb("comb2", [P, TI, P])
        cT = sb("cT", [2 * E, N], F32R)
        r_sb = xT
        r_hi = sb("r_hi", [P, FC, N], F32R)
        r_lo = sb("r_lo", [P, FC, N], F32R)
        gate_bc = w_sel[:, 0:2, :, :].rearrange("p q b k -> p q (b k)")
        yg = sb("yg", [P, N])
        acc = sb("acc", [P, N])

        zb = [bank(f"zb{i}") for i in range(LEAD)]
        yb = [bank(f"yb{i}") for i in range(2)]
        bA = bank("bA")
        bB = bank("bB")
        bG = bank("bG")
        hid_ps = [yb[1][:, 0:S], bB[:, 0:S], zb[0][:, 0:S], zb[1][:, 0:S]]
        se_ps, hyp1_ps, hyp2_ps, sty1_ps = bG[0:SE, 0:B], bG[:, 0:B], bG[:, 0:B], bG[0:HALF, 0:B]
        gz_ps, bz_ps = bG[:, 0:B], bG[:, B:2 * B]
        v_ps = zb[2][0:A, 0:B]
        M_ps = [bG[:, 0:D], yb[0][:, 0:(G - 1) * D]]

        ld_x = [sem(f"ld_x{g}") for g in range(2)]
        ld_xt = [sem(f"ld_xt{g}") for g in range(2)]
        ld_ids, ld_adapt, ld_style, ld_route = sem("ld_ids"), sem("ld_adapt"), sem("ld_style"), sem("ld_route")
        W_LOADS = [(0, 1), (1, 2), (2, 3), (3, 4), (4, 6), (6, 8)]
        ld_w = [sem(f"ld_w{i}") for i in range(len(W_LOADS))]
        zeros_done = sem("zeros_done")
        ones_done = sem("ones_done")
        pool_setup = sem("pool_setup")
        dve_setup = sem("dve_setup")
        subj_onehot = sem("subj_onehot")
        sel_done = sem("sel_done")
        down_done = sem("down_done")
        hid_done = sem("hid_done")
        w_sel_done, oh_done, rest_done = sem("w_sel_done"), sem("oh_done"), sem("rest_done")
        v_done, M_done, M2_done = sem("v_done"), sem("M_done"), sem("M2_done")
        style_mm, style_ev = sem("style_mm"), sem("style_ev")
        gexp_done, gln_done, gamma_done = sem("gexp_done"), sem("gln_done"), sem("gamma_done")
        whi_done, wlo_done = sem("whi_done"), sem("wlo_done")
        wlo_pool_done = sem("wlo_pool_done")
        b2_done = sem("b2_done")
        hid_cur_done, up_done, x0_done = sem("hid_cur_done"), sem("up_done"), sem("x0_done")
        var1, rstd1, x1_done = sem("var1"), sem("rstd1"), sem("x1_done")
        var2, rstd2, hn_done, hnT_done = sem("var2"), sem("rstd2"), sem("hn_done"), sem("hnT_done")
        var3, shift_done, aff_done, h2_done = sem("var3"), sem("shift_done"), sem("aff_done"), sem("h2_done")
        h2hi_done, h2lo_done = sem("h2hi_done"), sem("h2lo_done")
        logits_done, lsh_done, lex_done, comb_done = (
            sem("logits_done"), sem("lsh_done"), sem("lex_done"), sem("comb_done"))
        combT_done, cT_done, b2t_done, acc_init = (
            sem("combT_done"), sem("cT_done"), sem("b2t_done"), sem("acc_init"))
        dve_front, pool_front = sem("dve_front"), sem("pool_front")
        z_done, r_done = sem("z_done"), sem("r_done")
        hi_done = {k: sem(f"hi_done_{k}") for k in ("act", "dve", "pool")}
        lo_done, l2_done = sem("lo_done"), sem("l2_done")
        gate_mm, gate_done, yg_done, acc_done = (
            sem("gate_mm"), sem("gate_done"), sem("yg_done"), sem("acc_done"))
        fin_done, out_done, stored = sem("fin_done"), sem("out_done"), sem("stored")

        def need(eng, s, value):
            if isinstance(value, int) and value <= 0:
                return
            eng.wait_ge(s, value)

        def need_apart(eng, s, value):
            if isinstance(value, int):
                need(eng, s, value)
                return
            value = eng.to_reg(value)
            eng.wait_ge(ld_adapt, 16)
            eng.wait_ge(s, value)

        def his(kind, f):
            return sum(k == kind for k in HI_ENGINE[:f])

        def chunk(t, s):
            return t + s // CH, (s % CH) // FC, s % FC

        def each_slot(step, t, first, last):
            for s in range(first, last):
                step(t, s)

        def whole(run, eng):
            each_slot(run, 0, 0, SPLIT_AT)
            with eng.Fori(0, G - 1) as t:
                each_slot(run, t, SPLIT_AT, CH)
                each_slot(run, t + 1, 0, SPLIT_AT)
            each_slot(run, G - 1, SPLIT_AT, CH)

        def in_loop(t):
            return not isinstance(t, int)

        block = ctx.enter_context(nc.Block())

        @block.sync
        def _(sp):
            def load_w(i):
                a, b = W_LOADS[i]
                sp.dma_start(w1_sb[:, a:b, :], w1[:, a:b, :]).then_inc(ld_w[i], 16)
                sp.dma_start(w2_sb[:, a:b, :, :], w2[:, a:b, :, :]).then_inc(ld_w[i], 16)

            sp.dma_start(xT[:, 0, :], x_t[:, 0, :]).then_inc(ld_xt[0], 16)
            x_v = x.rearrange("b s d -> (b s) d").rearrange("(g i p) d -> p g i d", g=G, p=P)
            sp.dma_start(x_sb[:, 0, :, :], x_v[:, 0]).then_inc(ld_x[0], 16)
            sp.dma_start(xT[:, 1:G, :], x_t[:, 1:G, :]).then_inc(ld_xt[1], 16)
            load_w(0)
            load_w(1)
            sp.dma_start(x_sb[:, 1:G, :, :].rearrange("p g i d -> p (g i) d"),
                         x_v[:, 1:G].rearrange("p g i d -> p (g i) d")).then_inc(ld_x[1], 16)
            for i in range(2, len(W_LOADS)):
                load_w(i)
            out_v = out.rearrange("b s d -> (b s) d").rearrange("(g i p) d -> p g i d", g=G, p=P)

            def store(t):
                need(sp, out_done, t + 1)
                sp.dma_start(out_v[:, bass.ds(t, 1)], x1[:, bass.ds(t, 1)]).then_inc(stored, 16)
            with sp.Fori(0, G - 1) as t:
                store(t)
            store(G - 1)
            sp.wait_ge(stored, 16 * G)

        @block.gpsimd
        def _(pool):
            gp = nc.gpsimd
            n_setup = [0]

            def link(ins):
                n_setup[0] += 1
                ins.then_inc(pool_setup, 1)
                pool.wait_ge(pool_setup, n_setup[0])

            gp.memset(w_sel[:, :, :, :], 0.0).then_inc(zeros_done, 1)
            gp.memset(rest[:, :, :], 0.0).then_inc(zeros_done, 1)
            gp.memset(M2[:, :, :], 0.0).then_inc(zeros_done, 1)
            gp.memset(hid_cur[:, :], 0.0).then_inc(zeros_done, 1)
            pool.wait_ge(ld_ids, 16)
            link(gp.tensor_copy(sub_f[:, :], ids_sb[0:NSUBJ, B:2 * B]))
            link(gp.tensor_scalar(sub_w[:, :], sub_f[:, :], 0.0, float(NSUBJ), ALU.is_lt, ALU.mult))
            link(gp.tensor_tensor(sub_w[:, :], sub_w[:, :], sub_f[:, :], ALU.add))
            link(gp.tensor_scalar(sub_w[:, :], sub_w[:, :], 0.0, float(NSUBJ - 1), ALU.max, ALU.min))
            pool.wait_ge(ld_adapt, 16)
            gp.tensor_scalar(oh_s[:, :], sub_w[:, :], pid, None, ALU.is_equal).then_inc(subj_onehot, 1)
            link(gp.tensor_tensor(ln_g2[:, :], cols[:, COL_LN_G:COL_LN_G + 1], cols[:, COL_LN_G:COL_LN_G + 1], ALU.mult))
            link(gp.memset(minus_half[:, :], -0.5))
            gp.memset(comb2[:, :, :], 0.0).then_inc(zeros_done, 1)

            FRONT_LINKS = 6
            n_front = [0]

            def begin(T):
                n_front[0] = 0
                if in_loop(T):
                    pool.sem_clear(pool_front)

            def flink(ins):
                n_front[0] += 1
                ins.then_inc(pool_front, 1)
                pool.wait_ge(pool_front, n_front[0])

            def rstd_tokens(T, var, done):
                need_apart(pool, var, T + 1)
                flink(gp.tensor_scalar(ve[:, :], mv[:, :, 1], LN_EPS, None, ALU.add))
                gp.tensor_tensor(rstd[:, :], ve[:, :], minus_half[:, :], ALU.pow).then_inc(done, 1)

            def style_affine(T):
                need_apart(pool, var3, T + 1)
                flink(gp.tensor_scalar(ve_t[:, :], mv_t[:, :, 1], ln_g2[:, :], T_EPS, ALU.mult, ALU.add))
                flink(gp.tensor_tensor(rstd_t[:, :], ve_t[:, :], minus_half[:, 0:GB], ALU.pow))
                if not in_loop(T):
                    pool.wait_ge(gamma_done, 2)
                flink(gp.tensor_tensor(gain_t[:, :], rstd_t[:, :], gamma[:, bass.ds(T * GB, GB)], ALU.mult))
                need(pool, shift_done, T + 1)
                flink(gp.tensor_tensor(gb_t[:, :], gain_t[:, :], shift_t[:, :], ALU.mult))
                gp.tensor_scalar(aff_s[:, :], gain_t[:, :], cols[:, COL_LN_G:COL_LN_G + 1], None, ALU.mult)
                gp.tensor_tensor(aff_b[:, :], gb_t[:, :], beta[:, bass.ds(T * GB, GB)], ALU.add).then_inc(aff_done, 1)

            def accumulate(t, u):
                if u < 0:
                    t, u = t - 1, u + E
                n = E * t + u
                if u == 0:
                    need(pool, acc_init, t + 1)
                need(pool, yg_done, n + 1)
                need(pool, acc_done, n)
                gp.tensor_tensor(acc[:, :], acc[:, :], yg[:, :], ALU.add).then_inc(acc_done, 1)

            def fronts(T, s):
                if s == 10:
                    begin(T)
                    rstd_tokens(T, var1, rstd1)
                if s == 15:
                    rstd_tokens(T, var2, rstd2)
                if s == 20:
                    style_affine(T)

            def split_lo(e):
                i = next(i for i, (a, b) in enumerate(W_LOADS) if a <= e < b)
                pool.wait_ge(ld_w[i], 32)
                pool.wait_ge(whi_done, 2 * e + 2)
                gp.tensor_tensor(w2_lo[:, e], w2_sb[:, e], w2_hi[:, e].bitcast(F32), ALU.subtract)\
                  .then_inc(wlo_pool_done, 1)

            rstd_tokens(0, var1, rstd1)
            rstd_tokens(0, var2, rstd2)
            split_lo(0)
            style_affine(0)
            split_lo(1)
            assert n_front[0] == FRONT_LINKS

            def run(t, s):
                first = not in_loop(t) and t == 0
                if first and s + 2 < E:
                    split_lo(s + 2)
                if in_loop(t) and s >= SPLIT_AT:
                    fronts(t + 1, s)
                if s % FC == 1 and not (first and s < FC):
                    accumulate(t, s // FC - 1)
            whole(run, pool)
            accumulate(G - 1, E - 1)

        @block.scalar
        def _(act):
            sc = nc.scalar
            act.dma_start(adapt_sb[:, :], adapt).then_inc(ld_adapt, 16)
            act.dma_start(ids_sb[:, :], ids).then_inc(ld_ids, 16)
            act.dma_start(style_sb[:, :], style).then_inc(ld_style, 16)
            act.dma_start(route_sb[:, :], route).then_inc(ld_route, 16)

            def gelu(g):
                act.wait_ge(down_done, g + 1)
                for j in range(GB):
                    r = slice(HALF * j, HALF * j + A)
                    sc.activation(hid[r, g, :] if g else hid_cur[r, :], hid_ps[g][r, :], ACT.Gelu,
                                  bias=cols[r, COL_DOWN_B:COL_DOWN_B + 1]).then_inc(hid_done, 1)
            sc.preload_act_table(ACT.Gelu)
            act.wait_ge(ld_adapt, 16)
            act.wait_ge(zeros_done, 4)
            for g in range(G):
                gelu(g)
            act.wait_ge(ld_route, 16)
            sc.activation(sel[:, :, :], sel_f.rearrange("k (e p) -> k e p", e=E), ACT.Copy).then_inc(sel_done, 1)

            def split_hi(e):
                i = next(i for i, (a, b) in enumerate(W_LOADS) if a <= e < b)
                act.wait_ge(ld_w[i], 32)
                sc.activation(w1_hi[:, e, :], w1_sb[:, e, :], ACT.Copy).then_inc(whi_done, 1)
                sc.activation(w2_hi[:, e], w2_sb[:, e], ACT.Copy).then_inc(whi_done, 1)

            def apply_style(T):
                need(act, aff_done, T + 1)
                for j in range(GB):
                    sc.activation(h2[:, j * S:(j + 1) * S], bA[:, j * S:(j + 1) * S], ACT.Identity,
                                  bias=aff_b[:, j:j + 1], scale=aff_s[:, j:j + 1]).then_inc(h2_done, 1)

            def h2_round(T):
                need(act, h2_done, GB * (T + 1))
                dst = h2_hi[:, bass.ds(T, 1), :].rearrange("p o n -> p (o n)") if in_loop(T) else h2_hi[:, T, :]
                sc.activation(dst, h2[:, :], ACT.Copy).then_inc(h2hi_done, 1)

            def softmax_exp(T):
                need(act, lsh_done, T + 1)
                sc.activation(lex[:, :, :], lsh[:, :, :], ACT.Exp).then_inc(lex_done, 1)

            def take_cT(T):
                need(act, combT_done, T + 1)
                sc.activation(cT[:, :], bB[0:2 * E, :], ACT.Copy).then_inc(cT_done, 1)

            def init_acc(T):
                need(act, b2t_done, T + 1)
                need(act, fin_done, T)
                sc.activation(acc[:, :], bB[:, :], ACT.Copy).then_inc(acc_init, 1)

            def relu(t, s):
                T, e, f = chunk(t, s)
                n = CH * T + s % CH
                need(act, z_done, n + 1)
                need(act, lo_done, n - FC + 1)
                sc.activation(r_sb[:, f, :], zb[s % CH % LEAD][:, :], ACT.Relu,
                              bias=cols[:, e * FC + f:e * FC + f + 1]).then_inc(r_done, 1)
                if HI_ENGINE[f] == "act":
                    need(act, l2_done, n - FC + 1)
                    need(act, r_done, n + 1)
                    sc.activation(r_hi[:, f, :], r_sb[:, f, :], ACT.Copy).then_inc(hi_done["act"], 1)

            def take_gate(t, u):
                n = E * t + u
                need(act, gate_mm, n + 1)
                need(act, yg_done, n - 1)
                sc.activation(gate_bc[:, u % 2, :], bG[:, :], ACT.Copy).then_inc(gate_done, 1)

            split_hi(0)
            act.wait_ge(style_ev, 5)
            sc.activation(gexp[:, :], gabs[:, :], ACT.Exp, scale=-1.0).then_inc(gexp_done, 1)
            act.wait_ge(gexp_done, 1)
            sc.activation(gln[:, :], gexp[:, :], ACT.Ln, bias=1.0).then_inc(gln_done, 1)
            split_hi(1)
            apply_style(0)
            h2_round(0)
            for s in range(LEAD):
                relu(0, s)
            softmax_exp(0)

            def run(t, s):
                first = not in_loop(t) and t == 0
                if first and s + 2 < E:
                    split_hi(s + 2)
                if not (not in_loop(t) and t == G - 1 and s + LEAD >= CH):
                    relu(t, s + LEAD)
                if s == 1 and first:
                    take_cT(0)
                if s % FC == 3:
                    take_gate(t, s // FC)
                if s == 4:
                    init_acc(t)
                if in_loop(t) and s >= SPLIT_AT:
                    if s == 21:
                        apply_style(t + 1)
                    if s == 22:
                        h2_round(t + 1)
                    if s == 25:
                        softmax_exp(t + 1)
                    if s == 31:
                        take_cT(t + 1)
            whole(run, act)

        @block.vector
        def _(dve):
            v = nc.vector
            n_setup = [0]

            def link(ins):
                n_setup[0] += 1
                ins.then_inc(dve_setup, 1)
                dve.wait_ge(dve_setup, n_setup[0])

            def split_lo(e):
                i = next(i for i, (a, b) in enumerate(W_LOADS) if a <= e < b)
                dve.wait_ge(ld_w[i], 32)
                dve.wait_ge(whi_done, 2 * e + 1)
                v.tensor_tensor(w1_lo[:, e, :], w1_sb[:, e, :], w1_hi[:, e, :].bitcast(F32), ALU.subtract)\
                 .then_inc(wlo_done, 1)

            dve.wait_ge(ld_ids, 16)
            link(v.tensor_copy(dom_f[:, :], ids_sb[:, 0:B]))
            link(v.tensor_scalar(dom_c[:, :], dom_f[:, :], 0.0, float(NDOM - 1), ALU.max, ALU.min))
            dve.wait_ge(ld_adapt, 16)
            v.tensor_scalar(oh_d[:, :], dom_c[0:NDOM, :], pid[0:NDOM, :], None, ALU.is_equal)
            v.tensor_tensor(is_e[:, :, :], dom_c[:, None, :].to_broadcast([P, 4, B]),
                            eid[:, :, None].to_broadcast([P, 4, B]), ALU.is_equal)
            link(v.tensor_tensor(valid[:, :], dom_f[:, :], dom_c[:, :], ALU.is_equal))
            v.tensor_tensor(oh_v[:, :], oh_d[:, :], valid[0:NDOM, :], ALU.mult).then_inc(oh_done, 1)
            v.tensor_tensor(m_e[:, :, :], is_e[:, :, :], valid[:, None, :].to_broadcast([P, 4, B]), ALU.mult)
            link(v.tensor_scalar(inval[:, :], valid[0:A, :], -1.0, 1.0, ALU.mult, ALU.add))

            def select(b0, b1):
                for q in range(4):
                    last = v.tensor_tensor(w_sel[:, q, b0:b1, 0:A], ew_sb[:, q, None, :].to_broadcast([P, b1 - b0, A]),
                                           m_e[:, q, b0:b1, None].to_broadcast([P, b1 - b0, A]), ALU.mult)
                last.then_inc(w_sel_done, 1)
            dve.wait_ge(zeros_done, 4)
            select(0, GB)
            v.tensor_tensor(rest[0:A, :, 0:A], ident[0:A, None, 0:A].to_broadcast([A, B, A]),
                            inval[:, :, None].to_broadcast([A, B, A]), ALU.mult)
            v.memset(rest[A:A + 1, :, A:A + 1], 1.0)
            dve.wait_ge(v_done, 1)
            v.tensor_copy(rest[0:A, :, A], v_ps).then_inc(rest_done, 1)
            v.memset(hid_cur[A:A + 1, :], 1.0)
            v.memset(hid_cur[HALF + A:HALF + A + 1, :], 1.0).then_inc(ones_done, 1)

            def take_M(g0, g1, ps):
                for j in range(GB):
                    r = slice(HALF * j, HALF * (j + 1))
                    last = v.tensor_copy(M2[r, g0:g1, j * D:(j + 1) * D], ps[r, :].rearrange("p (g d) -> p g d", d=D))
                last.then_inc(M2_done, 1)
            dve.wait_ge(M_done, 1)
            take_M(0, 1, M_ps[0])
            select(GB, B)

            FRONT_LINKS = 17
            n_front = [0]

            def begin(T):
                n_front[0] = 0
                if in_loop(T):
                    dve.sem_clear(dve_front)

            def flink(ins):
                n_front[0] += 1
                ins.then_inc(dve_front, 1)
                dve.wait_ge(dve_front, n_front[0])

            def load_hid(T):
                for j in range(GB):
                    r = slice(HALF * j, HALF * j + A)
                    need_apart(dve, up_done, T)
                    last = v.tensor_copy(hid_cur[r, :], hid[r, bass.ds(T, 1), :].rearrange("p o n -> p (o n)"))
                last.then_inc(hid_cur_done, 1)

            def add_residual(T):
                need(dve, up_done, T + 1)
                src = x_sb[:, bass.ds(T, 1), :, :].rearrange("p o (c h) d -> p (o c) h d", c=GB) if in_loop(T) \
                    else x_sb[:, T, :, :].rearrange("p (c h) d -> p c h d", c=GB)
                v.tensor_tensor(x0[:, :, :].rearrange("p (c h) d -> p c h d", c=GB),
                                bA[:, :].rearrange("p (h c d) -> p c h d", h=S // P, c=GB), src,
                                ALU.add).then_inc(x0_done, 1)

            def moments(src):
                for i in range(TI):
                    last = v.bn_stats(st[:, i, :], src(i))
                flink(last)

            def aggregate(done):
                for i in range(TI):
                    last = v.bn_aggr(mv[:, i, :], st[:, i, :])
                last.then_inc(done, 1)

            def centre(T):
                if not in_loop(T):
                    dve.wait_ge(ld_style, 16)
                need(dve, var1, T + 1)
                for i in range(TI):
                    last = v.scalar_tensor_tensor(xg[:, i, :], x0[:, i, :], mv[:, i, 0:1], lng_bc, ALU.subtract, ALU.mult)
                flink(last)

            def x1_tile(T, i):
                return x1[:, bass.ds(T, 1), i, :].rearrange("p o d -> p (o d)") if in_loop(T) else x1[:, T, i, :]

            def scale(T):
                need(dve, rstd1, T + 1)
                for i in range(TI):
                    last = v.scalar_tensor_tensor(x1_tile(T, i), xg[:, i, :], rstd[:, i:i + 1], lnb_bc, ALU.mult, ALU.add)
                last.then_inc(x1_done, 1)

            def normalise(T, tiles):
                need_apart(dve, rstd2, T + 1)
                for i in tiles:
                    last = v.tensor_scalar(hn[:, i, :], x1_tile(T, i), mv[:, i, 0:1], rstd[:, i:i + 1],
                                           ALU.subtract, ALU.mult)
                if TI - 1 in tiles:
                    last.then_inc(hn_done, 1)

            def stats_over_time(T):
                need_apart(dve, hnT_done, T + 1)
                for j in range(GB):
                    last = v.bn_stats(st_t[:, j, :], bA[:, j * S:(j + 1) * S])
                flink(last)
                for j in range(GB):
                    last = v.bn_aggr(mv_t[:, j, :], st_t[:, j, :])
                last.then_inc(var3, 1)
                need(dve, var3, T + 1)
                g, b = cols[:, COL_LN_G:COL_LN_G + 1], cols[:, COL_LN_B:COL_LN_B + 1]
                flink(v.tensor_scalar(mean_t[:, :], mv_t[:, :, 0], g, b, ALU.mult, ALU.add))
                v.tensor_scalar(shift_t[:, :], mean_t[:, :], -1.0, b, ALU.mult, ALU.add).then_inc(shift_done, 1)

            def h2_rest(T):
                need(dve, h2hi_done, T + 1)
                if in_loop(T):
                    hi = h2_hi[:, bass.ds(T, 1), :].rearrange("p o n -> p (o n)")
                    lo = h2_lo[:, bass.ds(T, 1), :].rearrange("p o n -> p (o n)")
                else:
                    hi, lo = h2_hi[:, T, :], h2_lo[:, T, :]
                v.tensor_tensor(lo, h2[:, :], hi.bitcast(F32), ALU.subtract).then_inc(h2lo_done, 1)

            def softmax_shift(T):
                need(dve, logits_done, T + 1)
                lg = bB[:, 0:TI * E].rearrange("p (i e) -> p i e", i=TI)
                flink(v.tensor_reduce(lmax[:, :], lg, AX_X, ALU.max))
                v.tensor_tensor(lsh[:, :, :], lg, lmax[:, :, None].to_broadcast([P, TI, E]), ALU.subtract)\
                 .then_inc(lsh_done, 1)

            def probabilities(T):
                need(dve, lex_done, T + 1)
                flink(v.tensor_reduce(lsum[:, :], lex[:, :, :], AX_X, ALU.add))
                flink(v.reciprocal(lrec[:, :], lsum[:, :]))
                flink(v.tensor_tensor(prob[:, :, :], lex[:, :, :], lrec[:, :, None].to_broadcast([P, TI, E]), ALU.mult))

            def two_largest(T):
                for i in range(TI):
                    last = v.max(top[:, i, :], prob[:, i, :])
                flink(last)
                for i in range(TI):
                    last = v.max_index(top_i[:, i, :], top[:, i, :], prob[:, i, :])
                flink(last)

            def shares(T):
                v.tensor_copy(top_f[:, :, :], top_i[:, :, 0:2])
                flink(v.tensor_tensor(gsum[:, :], top[:, :, 0], top[:, :, 1], ALU.add))
                flink(v.reciprocal(grec[:, :], gsum[:, :]))
                v.tensor_tensor(oh0[:, :, :], iota_e[:, None, :].to_broadcast([P, TI, E]),
                                top_f[:, :, 0:1].to_broadcast([P, TI, E]), ALU.is_equal)
                v.tensor_tensor(oh1[:, :, :], iota_e[:, None, :].to_broadcast([P, TI, E]),
                                top_f[:, :, 1:2].to_broadcast([P, TI, E]), ALU.is_equal)
                flink(v.tensor_tensor(gate[:, :, :], top[:, :, 0:2], grec[:, :, None].to_broadcast([P, TI, 2]), ALU.mult))

            def combine(T):
                v.tensor_tensor(c0[:, :, :], oh0[:, :, :], gate[:, :, 0:1].to_broadcast([P, TI, E]), ALU.mult)
                flink(v.tensor_tensor(c1[:, :, :], oh1[:, :, :], gate[:, :, 1:2].to_broadcast([P, TI, E]), ALU.mult))
                flink(v.tensor_tensor(comb[:, :, :], c0[:, :, :], c1[:, :, :], ALU.add))
                if not in_loop(T):
                    dve.wait_ge(zeros_done, 5)
                flink(v.tensor_copy(comb2[:, :, 0:E].bitcast(F32R), comb[:, :, :]))
                v.tensor_tensor(comb2[:, :, E:2 * E], comb[:, :, :], comb2[:, :, 0:E], ALU.subtract)\
                 .then_inc(comb_done, 1)

            def round_hi(t, s):
                T, e, f = chunk(t, s)
                if HI_ENGINE[f] != "dve":
                    return
                n = CH * T + s % CH
                need(dve, r_done, n + 1)
                need(dve, l2_done, n - FC + 1)
                v.tensor_copy(r_hi[:, f, :], r_sb[:, f, :]).then_inc(hi_done["dve"], 1)

            def take_lo(t, s):
                T, e, f = chunk(t, s)
                n = CH * T + s % CH
                kind = HI_ENGINE[f]
                need(dve, hi_done[kind], (E * T + e) * his(kind, FC) + his(kind, f + 1))
                need(dve, l2_done, n - FC + 1)
                v.tensor_tensor(r_lo[:, f, :], r_sb[:, f, :], r_hi[:, f, :].bitcast(F32), ALU.subtract)\
                 .then_inc(lo_done, 1)

            def apply_gate(t, u):
                if u < 0:
                    t, u = t - 1, u + E
                n = E * t + u
                need(dve, l2_done, FC * (n + 1))
                need(dve, gate_done, n + 1)
                need(dve, acc_done, n)
                v.tensor_tensor(yg[:, :], yb[u % 2][:, :], gate_bc[:, u % 2, :], ALU.mult).then_inc(yg_done, 1)

            def finish(t):
                need(dve, fin_done, t + 1)
                res = x1[:, bass.ds(t, 1), :, :].rearrange("p o i d -> p (o i) d") if in_loop(t) else x1[:, t, :, :]
                v.tensor_tensor(res, bA[:, :].rearrange("p (i d) -> p i d", i=TI), res, ALU.add)\
                 .then_inc(out_done, 1)

            def style_step(n, out, ps, col, relu, rows=P):
                dve.wait_ge(style_mm, n)
                c = cols[0:rows, col:col + 1]
                if relu:
                    v.tensor_scalar(out[:, :], ps, c, 0.0, ALU.add, ALU.max).then_inc(style_ev, 1)
                else:
                    v.tensor_scalar(out[:, :], ps, c, None, ALU.add).then_inc(style_ev, 1)

            dve.wait_ge(style_mm, 1)
            v.tensor_copy(se_sb[:, :], se_ps).then_inc(style_ev, 1)
            begin(0)
            add_residual(0)
            dve.wait_ge(x0_done, 1)
            moments(lambda i: x0[:, i, :])
            aggregate(var1)
            style_step(2, hyp_h, hyp1_ps, COL_HYP_B1, True)
            centre(0)
            style_step(3, hyp_o, hyp2_ps, COL_HYP_B2, False)
            scale(0)
            dve.wait_ge(x1_done, 1)
            moments(lambda i: x1[:, 0, i, :])
            aggregate(var2)
            style_step(4, sty_h, sty1_ps, COL_STY_B1, True, HALF)
            dve.wait_ge(M_done, 2)
            take_M(1, G, M_ps[1])
            normalise(0, range(TI))
            dve.wait_ge(style_mm, 5)
            link(v.tensor_scalar(gz[:, :], gz_ps, cols[:, COL_GAMMA_B:COL_GAMMA_B + 1], None, ALU.add))
            v.scalar_tensor_tensor(gabs[:, :], gz[:, :], -1.0, gz[:, :], ALU.mult, ALU.max).then_inc(style_ev, 1)
            v.tensor_scalar(beta[:, :], bz_ps, cols[:, COL_BETA_B:COL_BETA_B + 1], None, ALU.add).then_inc(gamma_done, 1)
            stats_over_time(0)
            dve.wait_ge(gln_done, 1)
            link(v.scalar_tensor_tensor(gamma[:, :], gz[:, :], 0.0, gln[:, :], ALU.max, ALU.add))
            v.tensor_scalar(gamma[:, :], gamma[:, :], SOFTPLUS_EPS, None, ALU.add).then_inc(gamma_done, 1)
            split_lo(0)
            split_lo(1)
            h2_rest(0)
            softmax_shift(0)
            for s in range(LEAD):
                round_hi(0, s)
                take_lo(0, s)

            def run(t, s):
                first = not in_loop(t) and t == 0
                if first and s == 0:
                    probabilities(0)
                    two_largest(0)
                    shares(0)
                    combine(0)
                    assert n_front[0] == FRONT_LINKS, n_front
                    dve.wait_ge(ld_route, 16)
                    link(v.tensor_copy(b2_hi[:, :], b2_sb))
                    v.tensor_tensor(b2_lo[:, :], b2_sb, b2_hi[:, :].bitcast(F32), ALU.subtract).then_inc(b2_done, 1)
                if first and s + 2 < E:
                    split_lo(s + 2)
                if not (not in_loop(t) and t == G - 1 and s + LEAD >= CH):
                    round_hi(t, s + LEAD)
                    take_lo(t, s + LEAD)
                if s % FC == 0 and not (first and s == 0):
                    apply_gate(t, s // FC - 1)
                if s == 4 and not first:
                    finish(t - 1)
                if in_loop(t) and s >= SPLIT_AT:
                    T = t + 1
                    if s == 6:
                        load_hid(T)
                    if s == 8:
                        begin(T)
                        add_residual(T)
                    if s == 9:
                        need_apart(dve, x0_done, T + 1)
                        moments(lambda i: x0[:, i, :])
                    if s == 10:
                        aggregate(var1)
                    if s == 11:
                        centre(T)
                    if s == 12:
                        scale(T)
                    if s == 13:
                        need_apart(dve, x1_done, T + 1)
                        moments(lambda i: x1_tile(T, i))
                    if s == 14:
                        aggregate(var2)
                    if s == 16:
                        normalise(T, (0, 1))
                    if s == 17:
                        normalise(T, (2, 3))
                    if s == 19:
                        stats_over_time(T)
                    if s == 23:
                        h2_rest(T)
                    if s == 24:
                        softmax_shift(T)
                    if s == 26:
                        probabilities(T)
                    if s == 27:
                        two_largest(T)
                    if s == 28:
                        shares(T)
                    if s == 29:
                        combine(T)
                        assert n_front[0] == FRONT_LINKS, n_front
            whole(run, dve)
            apply_gate(G - 1, E - 1)
            finish(G - 1)

        @block.tensor
        def _(pe):
            te = nc.tensor

            def down(g):
                pe.wait_ge(ld_xt[min(g, 1)], 16)
                for j in range(GB):
                    last = te.matmul(hid_ps[g][HALF * j:HALF * j + A, :], down_T, xT[:, g, j * S:(j + 1) * S],
                                     start=True, stop=True)
                last.then_inc(down_done, 1)

            def choose(g, ps):
                seqs = slice(g * GB, (g + 1) * GB)
                for q in range(4):
                    te.matmul(ps, w_sel[:, q, seqs, :].rearrange("p c k -> p (c k)"), up_rep,
                              start=(q == 0), stop=False)
                return te.matmul(ps, rest[:, seqs, :].rearrange("p c k -> p (c k)"), up_ext, start=False, stop=True)

            pe.wait_ge(ld_adapt, 16)
            down(0)
            pe.wait_ge(oh_done, 1)
            te.matmul(v_ps, eb_sb, oh_v[:, :], start=True, stop=False)
            te.matmul(v_ps, demb_sb, oh_d[:, :], start=False, stop=True).then_inc(v_done, 1)
            pe.wait_ge(w_sel_done, 1)
            pe.wait_ge(rest_done, 1)
            choose(0, M_ps[0]).then_inc(M_done, 1)

            def up(T):
                if in_loop(T):
                    need(pe, hid_cur_done, T)
                else:
                    pe.wait_ge(hid_done, GB)
                if not (isinstance(T, int) and T == 0):
                    need(pe, lo_done, CH * (T - 1) + 5 + LEAD + 1)
                rhs = M2[:, bass.ds(T, 1), :].rearrange("p o n -> p (o n)") if in_loop(T) else M2[:, T, :]
                for h in range(S // P):
                    last = te.matmul(bA[:, h * GB * D:(h + 1) * GB * D], hid_cur[:, h * P:(h + 1) * P], rhs,
                                     start=True, stop=True)
                last.then_inc(up_done, 1)

            def transpose_hn(T):
                need(pe, hn_done, T + 1)
                for i in range(TI):
                    last = te.transpose(bA[:, i * P:(i + 1) * P], hn[:, i, :], ident)
                last.then_inc(hnT_done, 1)

            def logits(T):
                need(pe, h2_done, GB * (T + 1))
                need(pe, acc_init, T)
                for i in range(TI):
                    last = te.matmul(bB[:, i * E:(i + 1) * E], h2[:, i * P:(i + 1) * P], rw_sb,
                                     start=True, stop=True)
                last.then_inc(logits_done, 1)

            def transpose_comb(T):
                need(pe, comb_done, T + 1)
                for i in range(TI):
                    last = te.transpose(bB[:, i * P:(i + 1) * P], comb2[:, i, :], ident)
                last.then_inc(combT_done, 1)

            def bias2(T):
                need(pe, cT_done, T + 1)
                te.matmul(bB[:, :], b2_hi[:, :], cT[:, :], start=True, stop=False)
                te.matmul(bB[:, :], b2_lo[:, :], cT[:, :], start=False, stop=True).then_inc(b2t_done, 1)

            def gate_rows(t, u):
                need(pe, cT_done, t + 1)
                need(pe, gate_done, E * t + u)
                te.matmul(bG[:, :], sel[:, u, :], cT[:, :], start=True, stop=True).then_inc(gate_mm, 1)

            def finish(t):
                need(pe, acc_done, E * (t + 1))
                need(pe, h2_done, GB * (t + 2 if in_loop(t) or t < G - 1 else G))
                for i in range(TI):
                    last = te.transpose(bA[:, i * P:(i + 1) * P], acc[:, i * P:(i + 1) * P], ident)
                last.then_inc(fin_done, 1)

            def tokens(buf, T):
                return buf[:, bass.ds(T, 1), :].rearrange("p o n -> p (o n)") if in_loop(T) else buf[:, T, :]

            def product1(t, s):
                T, e, f = chunk(t, s)
                n = CH * T + s % CH
                need(pe, r_done, n - (2 if s % CH < 2 else LEAD) + 1)
                z = zb[s % CH % LEAD]
                w = slice(f * P, (f + 1) * P)
                te.matmul(z[:, :], w1_lo[:, e, w], tokens(h2_hi, T), start=True, stop=False)
                te.matmul(z[:, :], w1_hi[:, e, w], tokens(h2_lo, T), start=False, stop=False)
                te.matmul(z[:, :], w1_hi[:, e, w], tokens(h2_hi, T), start=False, stop=True).then_inc(z_done, 1)

            def product2(t, s):
                e, f = s // FC, s % FC
                n = CH * t + s
                need(pe, lo_done, n + 1)
                if f == 0:
                    need(pe, yg_done, E * t + e - 1)
                y = yb[e % 2]
                te.matmul(y[:, :], w2_lo[:, e, f, :], r_hi[:, f, :], start=(f == 0), stop=False)
                te.matmul(y[:, :], w2_hi[:, e, f, :], r_lo[:, f, :], start=False, stop=False)
                te.matmul(y[:, :], w2_hi[:, e, f, :], r_hi[:, f, :], start=False, stop=(f == FC - 1)).then_inc(l2_done, 1)

            down(1)
            pe.wait_ge(M2_done, 1)
            pe.wait_ge(ones_done, 1)
            up(0)
            pe.wait_ge(subj_onehot, 1)
            pe.wait_ge(ld_style, 16)
            te.matmul(se_ps, subj_sb, oh_s[:, :], start=True, stop=True).then_inc(style_mm, 1)
            down(2)
            pe.wait_ge(style_ev, 1)
            te.matmul(hyp1_ps, hw1_sb, se_sb[:, :], start=True, stop=True).then_inc(style_mm, 1)
            down(3)
            pe.wait_ge(style_ev, 2)
            te.matmul(hyp2_ps, hw2_sb, hyp_h[:, :], start=True, stop=True).then_inc(style_mm, 1)
            pe.wait_ge(w_sel_done, 2)
            for g in range(1, G):
                last = choose(g, M_ps[1][:, (g - 1) * D:g * D])
            last.then_inc(M_done, 1)
            pe.wait_ge(style_ev, 3)
            te.matmul(sty1_ps, sw1_sb, hyp_o[:, :], start=True, stop=True).then_inc(style_mm, 1)
            pe.wait_ge(style_ev, 4)
            te.matmul(gz_ps, sw2_sb[:, 0:D], sty_h[:, :], start=True, stop=True)
            te.matmul(bz_ps, sw2_sb[:, D:2 * D], sty_h[:, :], start=True, stop=True).then_inc(style_mm, 1)
            transpose_hn(0)
            pe.wait_ge(hid_done, GB * G)
            logits(0)
            pe.wait_ge(h2lo_done, 1)
            pe.wait_ge(wlo_done, 1)
            for s in range(LEAD):
                product1(0, s)

            def run(t, s):
                first = not in_loop(t) and t == 0
                if not (not in_loop(t) and t == G - 1 and s + LEAD >= CH):
                    if s + LEAD == CH:
                        need(pe, h2lo_done, t + 2)
                    if not in_loop(t) and t == 0 and (s + LEAD) % FC == 0:
                        pe.wait_ge(wlo_done, (s + LEAD) // FC + 1)
                    product1(t, s + LEAD)
                if not in_loop(t) and t == 0 and s % FC == 0:
                    pe.wait_ge(wlo_pool_done, s // FC + 1)
                product2(t, s)
                if s == 1 and first:
                    transpose_comb(0)
                    pe.wait_ge(b2_done, 1)
                    pe.wait_ge(sel_done, 1)
                if s == 2:
                    bias2(t)
                if s % FC == 2:
                    gate_rows(t, s // FC)
                if s == 3 and not (not in_loop(t) and t == 0):
                    finish(t - 1)
                if s == SPLIT_AT - 1 and not in_loop(t) and t == 0:
                    pe.wait_ge(wlo_done, E)
                    pe.wait_ge(wlo_pool_done, E)
                if in_loop(t) and s >= SPLIT_AT:
                    if s == 7:
                        up(t + 1)
                    if s == 18:
                        transpose_hn(t + 1)
                    if s == 23:
                        logits(t + 1)
                    if s == 31:
                        transpose_comb(t + 1)
            whole(run, pe)
            finish(G - 1)


def packed(parts, widths, rows):
    import numpy as np

    at, n = widths
    a = np.zeros((rows, n), np.float32)
    for name, (c0, c1) in at.items():
        p = parts[name]
        a[0:p.shape[0], c0:c1] = p
    return a


def kernel(**inputs):
    import numpy as np
    import concourse.bacc as bacc
    from concourse.bass_utils import run_bass_kernel_spmd

    p0 = {k.removeprefix("L0_cond_"): np.asarray(v) for k, v in inputs.items()}
    q = {k.removeprefix("L1_cond_"): np.asarray(v) for k, v in inputs.items()}
    x = np.ascontiguousarray(inputs["x"])
    cols = np.zeros((P, COLS), np.float32)
    cols[:, 0:CH] = q["exp_b1"].reshape(CH, P).T
    for c, v in ((COL_LN_G, q["ln_g"]), (COL_LN_B, q["ln_b"]), (COL_HYP_B1, q["hyp_b1"]), (COL_HYP_B2, q["hyp_b2"]),
                 (COL_GAMMA_B, q["sty_b2"][0:D]), (COL_BETA_B, q["sty_b2"][D:2 * D])):
        cols[:, c] = v
    cols[0:HALF, COL_STY_B1] = q["sty_b1"]
    for j in range(GB):
        cols[HALF * j:HALF * j + A, COL_DOWN_B] = p0["down_b"]
    adapt = packed({
        "down_T": p0["down_W"].T, "up_rep": np.tile(p0["up_W"].T, (4, 1)),
        "up_ext": np.concatenate([p0["up_W"].T, p0["up_b"][None, :]]),
        "experts": p0["expert_W"].reshape(4, P, A).transpose(1, 0, 2).reshape(P, 4 * A),
        "expert_b": p0["expert_b"], "domain_emb": p0["domain_emb"], "cols": cols,
        "ident": np.eye(P, dtype=np.float32),
        "eid": np.array([[(t * P + p) // A for t in range(4)] for p in range(P)], np.float32),
        "pid": np.arange(P, dtype=np.float32)[:, None],
        "iota_e": np.tile(np.arange(E, dtype=np.float32), (P, 1)),
    }, (ADAPT, ADAPT_N), P)
    style = packed({
        "subj": q["subj_emb"], "hyp_w1": q["hyp_w1"], "hyp_w2": q["hyp_w2"], "sty_w1": q["sty_w1"],
        "sty_w2": q["sty_w2"], "router_w": q["router_w"], "ln_gamma": np.tile(p0["ln_gamma"], (P, 1)),
        "ln_beta": np.tile(p0["ln_beta"], (P, 1)),
    }, (STYLE, STYLE_N), P)
    route = packed({
        "exp_b2": np.tile(q["exp_b2"], (2, 1)),
        "sel": np.tile(np.repeat(np.eye(E, dtype=np.float32), P, axis=1), (2, 1)),
    }, (ROUTE, ROUTE_N), 2 * E)
    arrays = {
        "x": x,
        "x_t": np.ascontiguousarray(x.reshape(B * S, D).T).reshape(D, G, N),
        "ids": np.tile(np.concatenate([inputs["itok_B_0_15"], inputs["itok_B_6_14"]])[None, :], (P, 1)),
        "adapt": adapt, "style": style, "route": route,
        "w1": np.ascontiguousarray(q["exp_w1"].transpose(1, 0, 2)),
        "w2": np.ascontiguousarray(q["exp_w2"].reshape(E, FC, P, D).transpose(2, 0, 1, 3)),
    }
    nc = bacc.Bacc("TRN2", target_bir_lowering=False, num_devices=1)
    args = [nc.dram_tensor(k, a.shape, mybir.dt.from_np(a.dtype), kind="ExternalInput").ap() for k, a in arrays.items()]
    args.append(nc.dram_tensor("result", (B, S, D), F32, kind="ExternalOutput").ap())
    program(nc, *args)
    return run_bass_kernel_spmd(nc, [arrays], core_ids=[0]).results[0]["result"]
```

```python
from contextlib import ExitStack

import concourse.bass as bass
from concourse import mybir

F32 = mybir.dt.float32
F32R = mybir.dt.float32r
I32 = mybir.dt.int32
U32 = mybir.dt.uint32
ALU = mybir.AluOpType
ACT = mybir.ActivationFunctionType
AX_X = mybir.AxisListType.X

P = 128
B, S, D = 8, 256, 128
A, NDOM = 32, 16
NSUBJ, SE = 32, 64
E, FF = 8, 512
GB = 2
G = B // GB
N = GB * S
TI = N // P
FC = FF // P
CH = E * FC
HALF = 64
STAGE = 4
NZ = 4
LEAD = 5
GR = 4
C_WHOLE = 32
C_ROWS = C_WHOLE + E
RB = 8
SPLIT_AT = 6
SPLIT_SLOTS = (0, 1, 3, 4)
LN_EPS, T_EPS, SOFTPLUS_EPS = 1e-5, 1e-8, 1e-8

COL_LN_G, COL_LN_B, COL_HYP_B1, COL_HYP_B2 = 32, 33, 34, 35
COL_GAMMA_B, COL_BETA_B, COL_STY_B1, COL_DOWN_B = 36, 37, 38, 39
COLS = 40


def packing(parts):
    at, n = {}, 0
    for name, width in parts:
        at[name] = (n, n + width)
        n += width
    return at, n


ADAPT, ADAPT_N = packing([("down_T", A), ("up_rep", D), ("up_ext", D), ("experts", 4 * A), ("expert_b", A),
                          ("domain_emb", A), ("cols", COLS), ("ident", P), ("eid", 4), ("pid", 1), ("iota_e", E)])
STYLE, STYLE_N = packing([("subj", SE), ("hyp_w1", P), ("hyp_w2", P), ("sty_w1", HALF), ("sty_w2", 2 * D),
                          ("router_w", E), ("ln_gamma", D), ("ln_beta", D), ("exp_b2", D)])

HI_ENGINE = ("act", "dve", "act", "dve")
LO_ENGINE = ("dve", "pool", "dve", "pool")


def program(nc, x, x_t, ids, adapt, style, w1, w2, out, gates):
    ctx = ExitStack()
    with ctx:
        def sb(name, shape, dt=F32):
            return ctx.enter_context(nc.sbuf_tensor(name, shape, dt))

        def bank(name):
            return ctx.enter_context(nc.psum_tensor(name, [P, 512], F32))

        def sem(name):
            return ctx.enter_context(nc.semaphore(name))

        ids_sb = sb("ids_sb", [P, 2 * B], I32)
        adapt_sb = sb("adapt_sb", [P, ADAPT_N])
        style_sb = sb("style_sb", [P, STYLE_N])

        def part(tile, at, name, rows=P):
            return tile[0:rows, at[name][0]:at[name][1]]

        down_T = part(adapt_sb, ADAPT, "down_T")
        up_rep = part(adapt_sb, ADAPT, "up_rep")
        up_ext = part(adapt_sb, ADAPT, "up_ext", A + 1)
        ew_sb = part(adapt_sb, ADAPT, "experts").rearrange("p (t a) -> p t a", t=4)
        eb_sb = part(adapt_sb, ADAPT, "expert_b", NDOM)
        demb_sb = part(adapt_sb, ADAPT, "domain_emb", NDOM)
        cols = part(adapt_sb, ADAPT, "cols")
        ident = part(adapt_sb, ADAPT, "ident")
        eid = part(adapt_sb, ADAPT, "eid")
        pid = part(adapt_sb, ADAPT, "pid", NSUBJ)
        iota_e = part(adapt_sb, ADAPT, "iota_e")
        subj_sb = part(style_sb, STYLE, "subj", NSUBJ)
        hw1_sb = part(style_sb, STYLE, "hyp_w1", SE)
        hw2_sb = part(style_sb, STYLE, "hyp_w2")
        sw1_sb = part(style_sb, STYLE, "sty_w1")
        sw2_sb = part(style_sb, STYLE, "sty_w2", HALF)
        rw_sb = part(style_sb, STYLE, "router_w")
        lng_bc = part(style_sb, STYLE, "ln_gamma")
        lnb_bc = part(style_sb, STYLE, "ln_beta")
        b2_sb = part(style_sb, STYLE, "exp_b2", 2 * E)
        b2_hi = sb("b2_hi", [2 * E, D], F32R)
        b2_lo = sb("b2_lo", [2 * E, D], F32R)
        w1_hi = sb("w1_hi", [P, E, FF], F32R)
        w1_lo = sb("w1_lo", [P, E, FF], F32R)
        w2_hi = sb("w2_hi", [P, E, FC, D], F32R)
        w2_lo = sb("w2_lo", [P, E, FC, D], F32R)
        w1_sb = sb("w1_sb", [P, STAGE, FF])
        w2_sb = sb("w2_sb", [P, STAGE, FC, D])
        minus_half = sb("minus_half", [P, TI])
        dom_f = sb("dom_f", [P, B])
        dom_c = sb("dom_c", [P, B])
        valid = sb("valid", [P, B])
        is_e = sb("is_e", [P, 4, B])
        m_e = sb("m_e", [P, 4, B])
        w_sel = sb("w_sel", [P, 4, B, HALF])
        rest = sb("rest", [A + 1, B, HALF])
        inval = sb("inval", [A, B])
        oh_d = sb("oh_d", [NDOM, B])
        oh_v = sb("oh_v", [NDOM, B])
        M2 = sb("M2", [P, G, GB * D])
        sub_f = sb("sub_f", [NSUBJ, B])
        sub_w = sb("sub_w", [NSUBJ, B])
        oh_s = sb("oh_s", [NSUBJ, B])
        se_sb = sb("se_sb", [SE, B])
        hyp_h = sb("hyp_h", [P, B])
        hyp_o = sb("hyp_o", [P, B])
        sty_h = sb("sty_h", [HALF, B])
        gz = sb("gz", [P, B])
        gabs = sb("gabs", [P, B])
        gexp = sb("gexp", [P, B])
        gln = sb("gln", [P, B])
        gamma = sb("gamma", [P, B])
        beta = sb("beta", [P, B])
        x_sb = sb("x_sb", [P, G, TI, D])
        r_sb = sb("r_sb", [P, RB, N])
        xT = r_sb[:, 0:G, :]
        hid = sb("hid", [P, G, S])
        hid_cur = sb("hid_cur", [P, S])
        x0 = sb("x0", [P, TI, D])
        st = sb("st", [P, TI, 6])
        mv = sb("mv", [P, TI, 2])
        ve = sb("ve", [P, TI])
        rstd = sb("rstd", [P, TI])
        xg = sb("xg", [P, TI, D])
        x1 = x_sb
        hn = xg
        ln_g2 = sb("ln_g2", [P, 1])
        mean_t = sb("mean_t", [P, GB])
        shift_t = sb("shift_t", [P, GB])
        gain_t = sb("gain_t", [P, GB])
        gb_t = sb("gb_t", [P, GB])
        st_t = sb("st_t", [P, GB, 6])
        mv_t = sb("mv_t", [P, GB, 2])
        ve_t = sb("ve_t", [P, GB])
        rstd_t = sb("rstd_t", [P, GB])
        aff_s = sb("aff_s", [P, GB])
        aff_b = sb("aff_b", [P, GB])
        h2 = sb("h2", [P, N])
        h2_hi = sb("h2_hi", [P, G, N], F32R)
        h2_lo = sb("h2_lo", [P, G, N], F32R)
        lmax = sb("lmax", [P, TI])
        lsh = sb("lsh", [P, TI, E])
        lex = sb("lex", [P, TI, E])
        lsum = sb("lsum", [P, TI])
        lrec = sb("lrec", [P, TI])
        prob = sb("prob", [P, TI, E])
        top = sb("top", [P, TI, 8])
        top_i = sb("top_i", [P, TI, 8], U32)
        top_f = sb("top_f", [P, TI, 2])
        gsum = sb("gsum", [P, TI])
        grec = sb("grec", [P, TI])
        gate = sb("gate", [P, TI, 2])
        oh0 = sb("oh0", [P, TI, E])
        oh1 = sb("oh1", [P, TI, E])
        c0 = sb("c0", [P, TI, E])
        c1 = sb("c1", [P, TI, E])
        comb = sb("comb", [P, TI, E])
        comb2 = sb("comb2", [P, TI, C_ROWS])
        cT = sb("cT", [2 * E, N], F32R)
        c_row = sb("c_row", [C_ROWS, N])
        gate_bc = sb("gate_bc", [P, GR, N])
        r_hi = sb("r_hi", [P, RB, N], F32R)
        r_lo = sb("r_lo", [P, RB, N], F32R)
        yg = sb("yg", [P, N])
        acc = sb("acc", [P, N])

        zb = [bank(f"zb{i}") for i in range(NZ)]
        yb = [bank(f"yb{i}") for i in range(2)]
        bA = bank("bA")
        bB = bank("bB")
        hid_ps = [yb[1][:, 0:S], bB[:, 0:S], zb[0][:, 0:S], zb[1][:, 0:S]]
        se_ps, hyp1_ps, hyp2_ps, sty1_ps = zb[3][0:SE, 0:B], zb[3][:, 0:B], zb[3][:, 0:B], zb[3][0:HALF, 0:B]
        gz_ps, bz_ps = zb[3][:, 0:B], zb[3][:, B:2 * B]
        v_ps = zb[2][0:A, 0:B]
        M_ps = [zb[3][:, 0:D], yb[0][:, 0:(G - 1) * D]]

        ld_x = [sem(f"ld_x{g}") for g in range(2)]
        ld_xt = [sem(f"ld_xt{g}") for g in range(2)]
        ld_ids, ld_adapt, ld_style = sem("ld_ids"), sem("ld_adapt"), sem("ld_style")
        ld_w = [sem(f"ld_w{i}") for i in range(STAGE)]
        zeros_done = sem("zeros_done")
        ones_done = sem("ones_done")
        pool_setup = sem("pool_setup")
        dve_setup = sem("dve_setup")
        subj_onehot = sem("subj_onehot")
        down_done = sem("down_done")
        hid_done = sem("hid_done")
        w_sel_done, oh_done, rest_done = sem("w_sel_done"), sem("oh_done"), sem("rest_done")
        v_done, M_done, M2_done = sem("v_done"), sem("M_done"), sem("M2_done")
        style_mm, style_ev = sem("style_mm"), sem("style_ev")
        gexp_done, gln_done, gamma_done = sem("gexp_done"), sem("gln_done"), sem("gamma_done")
        whi_done = sem("whi_done")
        wlo_pool, wlo_dve = sem("wlo_pool"), sem("wlo_dve")
        b2_done = sem("b2_done")
        hid_cur_done, up_done, x0_done = sem("hid_cur_done"), sem("up_done"), sem("x0_done")
        var1, rstd1, x1_done = sem("var1"), sem("rstd1"), sem("x1_done")
        var2, rstd2, hn_done, hnT_done = sem("var2"), sem("rstd2"), sem("hn_done"), sem("hnT_done")
        var3, shift_done, aff_done, h2_done = sem("var3"), sem("shift_done"), sem("aff_done"), sem("h2_done")
        h2hi_done, h2lo_done = sem("h2hi_done"), sem("h2lo_done")
        logits_done, lsh_done, lex_done, comb_done = (
            sem("logits_done"), sem("lsh_done"), sem("lex_done"), sem("comb_done"))
        combT_done, cT_done, c_row_done, b2t_done, acc_init = (
            sem("combT_done"), sem("cT_done"), sem("c_row_done"), sem("b2t_done"), sem("acc_init"))
        dve_front, pool_front = sem("dve_front"), sem("pool_front")
        z_done, r_done = sem("z_done"), sem("r_done")
        hi_done = {k: sem(f"hi_done_{k}") for k in ("act", "dve")}
        lo_done = {k: sem(f"lo_done_{k}") for k in ("dve", "pool")}
        l2_done = sem("l2_done")
        gates_out = sem("gates_out")
        gate_in = [sem(f"gate_in{i}") for i in range(GR)]
        yg_done, acc_done = sem("yg_done"), sem("acc_done")
        fin_done, out_done, stored = sem("fin_done"), sem("out_done"), sem("stored")

        def need(eng, s, value):
            if isinstance(value, int) and value <= 0:
                return
            eng.wait_ge(s, value)

        def need_apart(eng, s, value):
            if isinstance(value, int):
                need(eng, s, value)
                return
            value = eng.to_reg(value)
            eng.wait_ge(ld_adapt, 16)
            eng.wait_ge(s, value)

        def need_w(eng, e):
            eng.wait_ge(ld_w[e % STAGE], 32 * (e // STAGE + 1))

        def need_w1_lo(eng, e):
            if e < STAGE:
                eng.wait_ge(wlo_pool, 2 * e + 1)
            else:
                eng.wait_ge(wlo_dve, e - STAGE + 1)

        def need_w2_lo(eng, e):
            eng.wait_ge(wlo_pool, 2 * e + 2 if e < STAGE else STAGE + e + 1)

        def of_kind(engines, T, s):
            kind = engines[s % FC]
            return (CH * T + s) // FC * engines.count(kind) + engines[:s % FC + 1].count(kind) if isinstance(T, int) \
                else T * (E * engines.count(kind)) + (s // FC * engines.count(kind) + engines[:s % FC + 1].count(kind))

        def need_hi(eng, T, s):
            need(eng, hi_done[HI_ENGINE[s % FC]], of_kind(HI_ENGINE, T, s))

        def need_lo(eng, T, s):
            need(eng, lo_done[LO_ENGINE[s % FC]], of_kind(LO_ENGINE, T, s))

        def take_lo(engine, name, eng, t, s):
            if LO_ENGINE[s % FC] != name:
                return
            T, s = t + s // CH, s % CH
            b = s % RB
            need_hi(eng, T, s)
            engine.tensor_tensor(r_lo[:, b, :], r_sb[:, b, :], r_hi[:, b, :].bitcast(F32), ALU.subtract)\
                  .then_inc(lo_done[name], 1)

        def chunk(t, s):
            return t + s // CH, (s % CH) // FC, s % FC

        def each_slot(step, t, first, last):
            for s in range(first, last):
                step(t, s)

        def whole(run, eng):
            each_slot(run, 0, 0, SPLIT_AT)
            with eng.Fori(0, G - 1) as t:
                each_slot(run, t, SPLIT_AT, CH)
                each_slot(run, t + 1, 0, SPLIT_AT)
            each_slot(run, G - 1, SPLIT_AT, CH)

        def in_loop(t):
            return not isinstance(t, int)

        block = ctx.enter_context(nc.Block())

        @block.sync
        def _(sp):
            def load_w(e):
                if e >= STAGE:
                    need_w1_lo(sp, e - STAGE)
                sp.dma_start(w1_sb[:, e % STAGE], w1[:, e]).then_inc(ld_w[e % STAGE], 16)
                if e >= STAGE:
                    need_w2_lo(sp, e - STAGE)
                sp.dma_start(w2_sb[:, e % STAGE], w2[:, e]).then_inc(ld_w[e % STAGE], 16)

            sp.dma_start(xT[:, 0, :], x_t[:, 0, :]).then_inc(ld_xt[0], 16)
            x_v = x.rearrange("b s d -> (b s) d").rearrange("(g i p) d -> p g i d", g=G, p=P)
            sp.dma_start(x_sb[:, 0, :, :], x_v[:, 0]).then_inc(ld_x[0], 16)
            sp.dma_start(xT[:, 1:G, :], x_t[:, 1:G, :]).then_inc(ld_xt[1], 16)
            for e in range(STAGE):
                load_w(e)
            sp.dma_start(x_sb[:, 1:G, :, :].rearrange("p g i d -> p (g i) d"),
                         x_v[:, 1:G].rearrange("p g i d -> p (g i) d")).then_inc(ld_x[1], 16)
            for e in range(STAGE, E):
                load_w(e)
            out_v = out.rearrange("b s d -> (b s) d").rearrange("(g i p) d -> p g i d", g=G, p=P)

            def store(t):
                need(sp, out_done, t + 1)
                sp.dma_start(out_v[:, bass.ds(t, 1)], x1[:, bass.ds(t, 1)]).then_inc(stored, 16)

            def spread_gate(t, u):
                if u == 0:
                    need(sp, c_row_done, t + 1)
                    sp.dma_start(gates[:, bass.ds(t, 1), :], c_row[C_WHOLE:C_ROWS, None, :])\
                      .then_inc(gates_out, 16)
                    need(sp, gates_out, 16 * (t + 1))
                need(sp, yg_done, E * t + u - GR + 1)
                row = gates[u, bass.ds(t, 1), :].rearrange("o n -> (o n)")
                sp.dma_start(gate_bc[:, u % GR, :], row.partition_broadcast(P)).then_inc(gate_in[u % GR], 16)

            for u in range(E):
                spread_gate(0, u)
            with sp.Fori(1, G) as t:
                for u in range(GR):
                    spread_gate(t, u)
                store(t - 1)
                for u in range(GR, E):
                    spread_gate(t, u)
            store(G - 1)
            sp.wait_ge(stored, 16 * G)

        @block.gpsimd
        def _(pool):
            gp = nc.gpsimd
            n_setup = [0]

            def link(ins):
                n_setup[0] += 1
                ins.then_inc(pool_setup, 1)
                pool.wait_ge(pool_setup, n_setup[0])

            gp.memset(w_sel[:, :, :, :], 0.0).then_inc(zeros_done, 1)
            gp.memset(rest[:, :, :], 0.0).then_inc(zeros_done, 1)
            gp.memset(M2[:, :, :], 0.0).then_inc(zeros_done, 1)
            gp.memset(hid_cur[:, :], 0.0).then_inc(zeros_done, 1)
            gp.memset(comb2[:, :, 2 * E:C_WHOLE], 0.0).then_inc(zeros_done, 1)
            pool.wait_ge(ld_ids, 16)
            link(gp.tensor_copy(sub_f[:, :], ids_sb[0:NSUBJ, B:2 * B]))
            link(gp.tensor_scalar(sub_w[:, :], sub_f[:, :], 0.0, float(NSUBJ), ALU.is_lt, ALU.mult))
            link(gp.tensor_tensor(sub_w[:, :], sub_w[:, :], sub_f[:, :], ALU.add))
            link(gp.tensor_scalar(sub_w[:, :], sub_w[:, :], 0.0, float(NSUBJ - 1), ALU.max, ALU.min))
            pool.wait_ge(ld_adapt, 16)
            gp.tensor_scalar(oh_s[:, :], sub_w[:, :], pid, None, ALU.is_equal).then_inc(subj_onehot, 1)
            link(gp.tensor_tensor(ln_g2[:, :], cols[:, COL_LN_G:COL_LN_G + 1], cols[:, COL_LN_G:COL_LN_G + 1], ALU.mult))
            link(gp.memset(minus_half[:, :], -0.5))

            FRONT_LINKS = 6
            n_front = [0]

            def begin(T):
                n_front[0] = 0
                if in_loop(T):
                    pool.sem_clear(pool_front)

            def flink(ins):
                n_front[0] += 1
                ins.then_inc(pool_front, 1)
                pool.wait_ge(pool_front, n_front[0])

            def rstd_tokens(T, var, done):
                need_apart(pool, var, T + 1)
                flink(gp.tensor_scalar(ve[:, :], mv[:, :, 1], LN_EPS, None, ALU.add))
                gp.tensor_tensor(rstd[:, :], ve[:, :], minus_half[:, :], ALU.pow).then_inc(done, 1)

            def style_affine(T):
                need_apart(pool, var3, T + 1)
                flink(gp.tensor_scalar(ve_t[:, :], mv_t[:, :, 1], ln_g2[:, :], T_EPS, ALU.mult, ALU.add))
                flink(gp.tensor_tensor(rstd_t[:, :], ve_t[:, :], minus_half[:, 0:GB], ALU.pow))
                if not in_loop(T):
                    pool.wait_ge(gamma_done, 2)
                flink(gp.tensor_tensor(gain_t[:, :], rstd_t[:, :], gamma[:, bass.ds(T * GB, GB)], ALU.mult))
                need(pool, shift_done, T + 1)
                flink(gp.tensor_tensor(gb_t[:, :], gain_t[:, :], shift_t[:, :], ALU.mult))
                gp.tensor_scalar(aff_s[:, :], gain_t[:, :], cols[:, COL_LN_G:COL_LN_G + 1], None, ALU.mult)
                gp.tensor_tensor(aff_b[:, :], gb_t[:, :], beta[:, bass.ds(T * GB, GB)], ALU.add).then_inc(aff_done, 1)

            def accumulate(t, u):
                if u < 0:
                    t, u = t - 1, u + E
                n = E * t + u
                if u == 0:
                    need(pool, acc_init, t + 1)
                need(pool, yg_done, n + 1)
                need(pool, acc_done, n)
                gp.tensor_tensor(acc[:, :], acc[:, :], yg[:, :], ALU.add).then_inc(acc_done, 1)

            def fronts(T, s):
                if s == 10:
                    begin(T)
                    rstd_tokens(T, var1, rstd1)
                if s == 14:
                    rstd_tokens(T, var2, rstd2)
                if s == 20:
                    style_affine(T)

            def split_w1_lo(e):
                need_w(pool, e)
                pool.wait_ge(whi_done, 2 * e + 1)
                gp.tensor_tensor(w1_lo[:, e], w1_sb[:, e % STAGE], w1_hi[:, e].bitcast(F32), ALU.subtract)\
                  .then_inc(wlo_pool, 1)

            def split_w2_lo(e):
                need_w(pool, e)
                pool.wait_ge(whi_done, 2 * e + 2)
                gp.tensor_tensor(w2_lo[:, e], w2_sb[:, e % STAGE], w2_hi[:, e].bitcast(F32), ALU.subtract)\
                  .then_inc(wlo_pool, 1)

            split_w1_lo(0)
            rstd_tokens(0, var1, rstd1)
            split_w2_lo(0)
            split_w1_lo(1)
            rstd_tokens(0, var2, rstd2)
            split_w2_lo(1)
            split_w1_lo(2)
            style_affine(0)
            split_w2_lo(2)
            split_w1_lo(3)
            split_w2_lo(3)
            assert n_front[0] == FRONT_LINKS
            for s in range(LEAD):
                take_lo(gp, "pool", pool, 0, s)

            def run(t, s):
                first = not in_loop(t) and t == 0
                if in_loop(t) and s >= SPLIT_AT:
                    fronts(t + 1, s)
                if not (not in_loop(t) and t == G - 1 and s + LEAD >= CH):
                    take_lo(gp, "pool", pool, t, s + LEAD)
                if first and s in SPLIT_SLOTS:
                    split_w2_lo(STAGE + SPLIT_SLOTS.index(s))
                if s % FC == 1 and not (first and s < FC):
                    accumulate(t, s // FC - 1)
            whole(run, pool)
            accumulate(G - 1, E - 1)

        @block.scalar
        def _(act):
            sc = nc.scalar
            act.dma_start(ids_sb[:, :], ids).then_inc(ld_ids, 16)
            act.dma_start(adapt_sb[:, :], adapt).then_inc(ld_adapt, 16)
            act.dma_start(style_sb[:, :], style).then_inc(ld_style, 16)

            def gelu(g):
                act.wait_ge(down_done, g + 1)
                for j in range(GB):
                    r = slice(HALF * j, HALF * j + A)
                    sc.activation(hid[r, g, :] if g else hid_cur[r, :], hid_ps[g][r, :], ACT.Gelu,
                                  bias=cols[r, COL_DOWN_B:COL_DOWN_B + 1]).then_inc(hid_done, 1)
            sc.preload_act_table(ACT.Gelu)
            act.wait_ge(ld_adapt, 16)
            act.wait_ge(zeros_done, 4)

            def split_hi(e):
                need_w(act, e)
                sc.activation(w1_hi[:, e, :], w1_sb[:, e % STAGE, :], ACT.Copy).then_inc(whi_done, 1)
                sc.activation(w2_hi[:, e], w2_sb[:, e % STAGE], ACT.Copy).then_inc(whi_done, 1)

            def apply_style(T):
                need(act, aff_done, T + 1)
                for j in range(GB):
                    sc.activation(h2[:, j * S:(j + 1) * S], bA[:, j * S:(j + 1) * S], ACT.Identity,
                                  bias=aff_b[:, j:j + 1], scale=aff_s[:, j:j + 1]).then_inc(h2_done, 1)

            def h2_round(T):
                need(act, h2_done, GB * (T + 1))
                dst = h2_hi[:, bass.ds(T, 1), :].rearrange("p o n -> p (o n)") if in_loop(T) else h2_hi[:, T, :]
                sc.activation(dst, h2[:, :], ACT.Copy).then_inc(h2hi_done, 1)

            def softmax_exp(T):
                need(act, lsh_done, T + 1)
                sc.activation(lex[:, :, :], lsh[:, :, :], ACT.Exp).then_inc(lex_done, 1)

            def take_cT(T):
                need(act, combT_done, T + 1)
                need(act, b2t_done, T)
                sc.activation(cT[:, :], bB[0:2 * E, :], ACT.Copy).then_inc(cT_done, 1)
                need(act, gates_out, 16 * T)
                sc.activation(c_row[C_WHOLE:C_ROWS, :], bB[C_WHOLE:C_ROWS, :], ACT.Copy).then_inc(c_row_done, 1)

            def init_acc(T):
                need(act, b2t_done, T + 1)
                need(act, fin_done, T)
                sc.activation(acc[:, :], bB[:, :], ACT.Copy).then_inc(acc_init, 1)

            def relu(t, s):
                T, s = t + s // CH, s % CH
                n, b = CH * T + s, s % RB
                need(act, z_done, n + 1)
                need(act, l2_done, n - RB + 1)
                sc.activation(r_sb[:, b, :], zb[s % NZ][:, :], ACT.Relu, bias=cols[:, s:s + 1]).then_inc(r_done, 1)
                if HI_ENGINE[s % FC] == "act":
                    need(act, r_done, n + 1)
                    sc.activation(r_hi[:, b, :], r_sb[:, b, :], ACT.Copy).then_inc(hi_done["act"], 1)

            gelu(0)
            split_hi(0)
            gelu(1)
            split_hi(1)
            gelu(2)
            gelu(3)
            sc.preload_act_table(ACT.Exp)
            split_hi(2)
            act.wait_ge(style_ev, 5)
            sc.activation(gexp[:, :], gabs[:, :], ACT.Exp, scale=-1.0).then_inc(gexp_done, 1)
            act.wait_ge(gexp_done, 1)
            sc.activation(gln[:, :], gexp[:, :], ACT.Ln, bias=1.0).then_inc(gln_done, 1)
            sc.preload_act_table(ACT.Exp)
            split_hi(3)
            apply_style(0)
            h2_round(0)
            softmax_exp(0)
            for s in range(LEAD):
                relu(0, s)

            def run(t, s):
                first = not in_loop(t) and t == 0
                if first and s in SPLIT_SLOTS:
                    split_hi(STAGE + SPLIT_SLOTS.index(s))
                if not (not in_loop(t) and t == G - 1 and s + LEAD >= CH):
                    relu(t, s + LEAD)
                if s == 0:
                    take_cT(t)
                if s == 5:
                    init_acc(t)
                if in_loop(t) and s >= SPLIT_AT:
                    if s == 21:
                        apply_style(t + 1)
                    if s == 22:
                        h2_round(t + 1)
                    if s == 26:
                        softmax_exp(t + 1)
            whole(run, act)

        @block.vector
        def _(dve):
            v = nc.vector
            n_setup = [0]

            def link(ins):
                n_setup[0] += 1
                ins.then_inc(dve_setup, 1)
                dve.wait_ge(dve_setup, n_setup[0])

            def split_lo(e):
                need_w(dve, e)
                dve.wait_ge(whi_done, 2 * e + 1)
                v.tensor_tensor(w1_lo[:, e, :], w1_sb[:, e % STAGE, :], w1_hi[:, e, :].bitcast(F32), ALU.subtract)\
                 .then_inc(wlo_dve, 1)

            dve.wait_ge(ld_ids, 16)
            link(v.tensor_copy(dom_f[:, :], ids_sb[:, 0:B]))
            link(v.tensor_scalar(dom_c[:, :], dom_f[:, :], 0.0, float(NDOM - 1), ALU.max, ALU.min))
            dve.wait_ge(ld_adapt, 16)
            v.tensor_scalar(oh_d[:, :], dom_c[0:NDOM, :], pid[0:NDOM, :], None, ALU.is_equal)
            v.tensor_tensor(is_e[:, :, :], dom_c[:, None, :].to_broadcast([P, 4, B]),
                            eid[:, :, None].to_broadcast([P, 4, B]), ALU.is_equal)
            link(v.tensor_tensor(valid[:, :], dom_f[:, :], dom_c[:, :], ALU.is_equal))
            v.tensor_tensor(oh_v[:, :], oh_d[:, :], valid[0:NDOM, :], ALU.mult).then_inc(oh_done, 1)
            v.tensor_tensor(m_e[:, :, :], is_e[:, :, :], valid[:, None, :].to_broadcast([P, 4, B]), ALU.mult)
            link(v.tensor_scalar(inval[:, :], valid[0:A, :], -1.0, 1.0, ALU.mult, ALU.add))

            def select(b0, b1):
                for q in range(4):
                    last = v.tensor_tensor(w_sel[:, q, b0:b1, 0:A], ew_sb[:, q, None, :].to_broadcast([P, b1 - b0, A]),
                                           m_e[:, q, b0:b1, None].to_broadcast([P, b1 - b0, A]), ALU.mult)
                last.then_inc(w_sel_done, 1)
            dve.wait_ge(zeros_done, 4)
            select(0, GB)
            v.tensor_tensor(rest[0:A, :, 0:A], ident[0:A, None, 0:A].to_broadcast([A, B, A]),
                            inval[:, :, None].to_broadcast([A, B, A]), ALU.mult)
            v.memset(rest[A:A + 1, :, A:A + 1], 1.0)
            dve.wait_ge(v_done, 1)
            v.tensor_copy(rest[0:A, :, A], v_ps).then_inc(rest_done, 1)
            v.memset(hid_cur[A:A + 1, :], 1.0)
            v.memset(hid_cur[HALF + A:HALF + A + 1, :], 1.0).then_inc(ones_done, 1)

            def take_M(g0, g1, ps):
                for j in range(GB):
                    r = slice(HALF * j, HALF * (j + 1))
                    last = v.tensor_copy(M2[r, g0:g1, j * D:(j + 1) * D], ps[r, :].rearrange("p (g d) -> p g d", d=D))
                last.then_inc(M2_done, 1)
            dve.wait_ge(M_done, 1)
            take_M(0, 1, M_ps[0])
            select(GB, B)

            FRONT_LINKS = 17
            n_front = [0]

            def begin(T):
                n_front[0] = 0
                if in_loop(T):
                    dve.sem_clear(dve_front)

            def flink(ins):
                n_front[0] += 1
                ins.then_inc(dve_front, 1)
                dve.wait_ge(dve_front, n_front[0])

            def load_hid(T):
                for j in range(GB):
                    r = slice(HALF * j, HALF * j + A)
                    need_apart(dve, up_done, T)
                    last = v.tensor_copy(hid_cur[r, :], hid[r, bass.ds(T, 1), :].rearrange("p o n -> p (o n)"))
                last.then_inc(hid_cur_done, 1)

            def add_residual(T):
                need(dve, up_done, T + 1)
                src = x_sb[:, bass.ds(T, 1), :, :].rearrange("p o (c h) d -> p (o c) h d", c=GB) if in_loop(T) \
                    else x_sb[:, T, :, :].rearrange("p (c h) d -> p c h d", c=GB)
                v.tensor_tensor(x0[:, :, :].rearrange("p (c h) d -> p c h d", c=GB),
                                bA[:, :].rearrange("p (h c d) -> p c h d", h=S // P, c=GB), src,
                                ALU.add).then_inc(x0_done, 1)

            def moments(src):
                for i in range(TI):
                    last = v.bn_stats(st[:, i, :], src(i))
                flink(last)

            def aggregate(done):
                for i in range(TI):
                    last = v.bn_aggr(mv[:, i, :], st[:, i, :])
                last.then_inc(done, 1)

            def centre(T):
                if not in_loop(T):
                    dve.wait_ge(ld_style, 16)
                need(dve, var1, T + 1)
                for i in range(TI):
                    last = v.scalar_tensor_tensor(xg[:, i, :], x0[:, i, :], mv[:, i, 0:1], lng_bc, ALU.subtract, ALU.mult)
                flink(last)

            def x1_tile(T, i):
                return x1[:, bass.ds(T, 1), i, :].rearrange("p o d -> p (o d)") if in_loop(T) else x1[:, T, i, :]

            def scale(T):
                need(dve, rstd1, T + 1)
                for i in range(TI):
                    last = v.scalar_tensor_tensor(x1_tile(T, i), xg[:, i, :], rstd[:, i:i + 1], lnb_bc, ALU.mult, ALU.add)
                last.then_inc(x1_done, 1)

            def normalise(T, tiles):
                need_apart(dve, rstd2, T + 1)
                for i in tiles:
                    last = v.tensor_scalar(hn[:, i, :], x1_tile(T, i), mv[:, i, 0:1], rstd[:, i:i + 1],
                                           ALU.subtract, ALU.mult)
                if TI - 1 in tiles:
                    last.then_inc(hn_done, 1)

            def stats_over_time(T):
                need_apart(dve, hnT_done, T + 1)
                for j in range(GB):
                    last = v.bn_stats(st_t[:, j, :], bA[:, j * S:(j + 1) * S])
                flink(last)
                for j in range(GB):
                    last = v.bn_aggr(mv_t[:, j, :], st_t[:, j, :])
                last.then_inc(var3, 1)
                need(dve, var3, T + 1)
                g, b = cols[:, COL_LN_G:COL_LN_G + 1], cols[:, COL_LN_B:COL_LN_B + 1]
                flink(v.tensor_scalar(mean_t[:, :], mv_t[:, :, 0], g, b, ALU.mult, ALU.add))
                v.tensor_scalar(shift_t[:, :], mean_t[:, :], -1.0, b, ALU.mult, ALU.add).then_inc(shift_done, 1)

            def h2_rest(T):
                need(dve, h2hi_done, T + 1)
                if in_loop(T):
                    hi = h2_hi[:, bass.ds(T, 1), :].rearrange("p o n -> p (o n)")
                    lo = h2_lo[:, bass.ds(T, 1), :].rearrange("p o n -> p (o n)")
                else:
                    hi, lo = h2_hi[:, T, :], h2_lo[:, T, :]
                v.tensor_tensor(lo, h2[:, :], hi.bitcast(F32), ALU.subtract).then_inc(h2lo_done, 1)

            def softmax_shift(T):
                need(dve, logits_done, T + 1)
                lg = bB[:, 0:TI * E].rearrange("p (i e) -> p i e", i=TI)
                flink(v.tensor_reduce(lmax[:, :], lg, AX_X, ALU.max))
                v.tensor_tensor(lsh[:, :, :], lg, lmax[:, :, None].to_broadcast([P, TI, E]), ALU.subtract)\
                 .then_inc(lsh_done, 1)

            def probabilities(T):
                need(dve, lex_done, T + 1)
                flink(v.tensor_reduce(lsum[:, :], lex[:, :, :], AX_X, ALU.add))
                flink(v.reciprocal(lrec[:, :], lsum[:, :]))
                flink(v.tensor_tensor(prob[:, :, :], lex[:, :, :], lrec[:, :, None].to_broadcast([P, TI, E]), ALU.mult))

            def two_largest(T):
                for i in range(TI):
                    last = v.max(top[:, i, :], prob[:, i, :])
                flink(last)
                for i in range(TI):
                    last = v.max_index(top_i[:, i, :], top[:, i, :], prob[:, i, :])
                flink(last)

            def shares(T):
                v.tensor_copy(top_f[:, :, :], top_i[:, :, 0:2])
                flink(v.tensor_tensor(gsum[:, :], top[:, :, 0], top[:, :, 1], ALU.add))
                flink(v.reciprocal(grec[:, :], gsum[:, :]))
                v.tensor_tensor(oh0[:, :, :], iota_e[:, None, :].to_broadcast([P, TI, E]),
                                top_f[:, :, 0:1].to_broadcast([P, TI, E]), ALU.is_equal)
                v.tensor_tensor(oh1[:, :, :], iota_e[:, None, :].to_broadcast([P, TI, E]),
                                top_f[:, :, 1:2].to_broadcast([P, TI, E]), ALU.is_equal)
                flink(v.tensor_tensor(gate[:, :, :], top[:, :, 0:2], grec[:, :, None].to_broadcast([P, TI, 2]), ALU.mult))

            def combine(T):
                v.tensor_tensor(c0[:, :, :], oh0[:, :, :], gate[:, :, 0:1].to_broadcast([P, TI, E]), ALU.mult)
                flink(v.tensor_tensor(c1[:, :, :], oh1[:, :, :], gate[:, :, 1:2].to_broadcast([P, TI, E]), ALU.mult))
                flink(v.tensor_tensor(comb[:, :, :], c0[:, :, :], c1[:, :, :], ALU.add))
                if not in_loop(T):
                    dve.wait_ge(zeros_done, 5)
                flink(v.tensor_copy(comb2[:, :, 0:E].bitcast(F32R), comb[:, :, :]))
                v.tensor_copy(comb2[:, :, C_WHOLE:C_ROWS], comb[:, :, :])
                v.tensor_tensor(comb2[:, :, E:2 * E], comb[:, :, :], comb2[:, :, 0:E], ALU.subtract)\
                 .then_inc(comb_done, 1)

            def round_hi(t, s):
                if HI_ENGINE[s % FC] != "dve":
                    return
                T, s = t + s // CH, s % CH
                n, b = CH * T + s, s % RB
                need(dve, r_done, n + 1)
                v.tensor_copy(r_hi[:, b, :], r_sb[:, b, :]).then_inc(hi_done["dve"], 1)

            def apply_gate(t, u):
                if u < 0:
                    t, u = t - 1, u + E
                n = E * t + u
                need(dve, l2_done, FC * (n + 1))
                need(dve, gate_in[u % GR], 16 * ((E // GR) * t + u // GR + 1))
                need(dve, acc_done, n)
                v.tensor_tensor(yg[:, :], yb[u % 2][:, :], gate_bc[:, u % GR, :], ALU.mult).then_inc(yg_done, 1)

            def finish(t):
                need(dve, fin_done, t + 1)
                res = x1[:, bass.ds(t, 1), :, :].rearrange("p o i d -> p (o i) d") if in_loop(t) else x1[:, t, :, :]
                v.tensor_tensor(res, bA[:, :].rearrange("p (i d) -> p i d", i=TI), res, ALU.add)\
                 .then_inc(out_done, 1)

            def style_step(n, out, ps, col, relu, rows=P):
                dve.wait_ge(style_mm, n)
                c = cols[0:rows, col:col + 1]
                if relu:
                    v.tensor_scalar(out[:, :], ps, c, 0.0, ALU.add, ALU.max).then_inc(style_ev, 1)
                else:
                    v.tensor_scalar(out[:, :], ps, c, None, ALU.add).then_inc(style_ev, 1)

            dve.wait_ge(style_mm, 1)
            v.tensor_copy(se_sb[:, :], se_ps).then_inc(style_ev, 1)
            begin(0)
            add_residual(0)
            dve.wait_ge(x0_done, 1)
            moments(lambda i: x0[:, i, :])
            aggregate(var1)
            style_step(2, hyp_h, hyp1_ps, COL_HYP_B1, True)
            centre(0)
            style_step(3, hyp_o, hyp2_ps, COL_HYP_B2, False)
            scale(0)
            dve.wait_ge(x1_done, 1)
            moments(lambda i: x1[:, 0, i, :])
            aggregate(var2)
            style_step(4, sty_h, sty1_ps, COL_STY_B1, True, HALF)
            dve.wait_ge(M_done, 2)
            take_M(1, G, M_ps[1])
            normalise(0, range(TI))
            dve.wait_ge(style_mm, 5)
            link(v.tensor_scalar(gz[:, :], gz_ps, cols[:, COL_GAMMA_B:COL_GAMMA_B + 1], None, ALU.add))
            v.scalar_tensor_tensor(gabs[:, :], gz[:, :], -1.0, gz[:, :], ALU.mult, ALU.max).then_inc(style_ev, 1)
            v.tensor_scalar(beta[:, :], bz_ps, cols[:, COL_BETA_B:COL_BETA_B + 1], None, ALU.add).then_inc(gamma_done, 1)
            stats_over_time(0)
            dve.wait_ge(gln_done, 1)
            link(v.scalar_tensor_tensor(gamma[:, :], gz[:, :], 0.0, gln[:, :], ALU.max, ALU.add))
            v.tensor_scalar(gamma[:, :], gamma[:, :], SOFTPLUS_EPS, None, ALU.add).then_inc(gamma_done, 1)
            link(v.tensor_copy(b2_hi[:, :], b2_sb))
            v.tensor_tensor(b2_lo[:, :], b2_sb, b2_hi[:, :].bitcast(F32), ALU.subtract).then_inc(b2_done, 1)
            h2_rest(0)
            softmax_shift(0)
            probabilities(0)
            two_largest(0)
            shares(0)
            combine(0)
            assert n_front[0] == FRONT_LINKS, n_front
            for s in range(LEAD):
                round_hi(0, s)
                take_lo(v, "dve", dve, 0, s)

            def run(t, s):
                first = not in_loop(t) and t == 0
                if first and s - 1 in SPLIT_SLOTS:
                    split_lo(STAGE + SPLIT_SLOTS.index(s - 1))
                if not (not in_loop(t) and t == G - 1 and s + LEAD >= CH):
                    round_hi(t, s + LEAD)
                    take_lo(v, "dve", dve, t, s + LEAD)
                if s % FC == 0 and not (first and s == 0):
                    apply_gate(t, s // FC - 1)
                if s == 5 and not first:
                    finish(t - 1)
                if in_loop(t) and s >= SPLIT_AT:
                    T = t + 1
                    if s == 6:
                        load_hid(T)
                    if s == 8:
                        begin(T)
                        add_residual(T)
                    if s == 9:
                        need_apart(dve, x0_done, T + 1)
                        moments(lambda i: x0[:, i, :])
                        aggregate(var1)
                    if s == 10:
                        centre(T)
                    if s == 12:
                        scale(T)
                    if s == 13:
                        need_apart(dve, x1_done, T + 1)
                        moments(lambda i: x1_tile(T, i))
                        aggregate(var2)
                    if s == 15:
                        normalise(T, (0, 1))
                    if s == 16:
                        normalise(T, (2, 3))
                    if s == 18:
                        stats_over_time(T)
                    if s == 23:
                        h2_rest(T)
                    if s == 25:
                        softmax_shift(T)
                    if s == 26:
                        probabilities(T)
                    if s == 27:
                        two_largest(T)
                    if s == 28:
                        shares(T)
                    if s == 29:
                        combine(T)
                        assert n_front[0] == FRONT_LINKS, n_front
            whole(run, dve)
            apply_gate(G - 1, E - 1)
            finish(G - 1)

        @block.tensor
        def _(pe):
            te = nc.tensor

            def down(g):
                pe.wait_ge(ld_xt[min(g, 1)], 16)
                for j in range(GB):
                    last = te.matmul(hid_ps[g][HALF * j:HALF * j + A, :], down_T, xT[:, g, j * S:(j + 1) * S],
                                     start=True, stop=True)
                last.then_inc(down_done, 1)

            def choose(g, ps):
                seqs = slice(g * GB, (g + 1) * GB)
                for q in range(4):
                    te.matmul(ps, w_sel[:, q, seqs, :].rearrange("p c k -> p (c k)"), up_rep,
                              start=(q == 0), stop=False)
                return te.matmul(ps, rest[:, seqs, :].rearrange("p c k -> p (c k)"), up_ext, start=False, stop=True)

            pe.wait_ge(ld_adapt, 16)
            down(0)
            pe.wait_ge(oh_done, 1)
            te.matmul(v_ps, eb_sb, oh_v[:, :], start=True, stop=False)
            te.matmul(v_ps, demb_sb, oh_d[:, :], start=False, stop=True).then_inc(v_done, 1)
            pe.wait_ge(w_sel_done, 1)
            pe.wait_ge(rest_done, 1)
            choose(0, M_ps[0]).then_inc(M_done, 1)

            def up(T):
                if in_loop(T):
                    need(pe, hid_cur_done, T)
                else:
                    pe.wait_ge(hid_done, GB)
                rhs = M2[:, bass.ds(T, 1), :].rearrange("p o n -> p (o n)") if in_loop(T) else M2[:, T, :]
                for h in range(S // P):
                    last = te.matmul(bA[:, h * GB * D:(h + 1) * GB * D], hid_cur[:, h * P:(h + 1) * P], rhs,
                                     start=True, stop=True)
                last.then_inc(up_done, 1)

            def transpose_hn(T):
                need(pe, hn_done, T + 1)
                for i in range(TI):
                    last = te.transpose(bA[:, i * P:(i + 1) * P], hn[:, i, :], ident)
                last.then_inc(hnT_done, 1)

            def logits(T):
                need(pe, h2_done, GB * (T + 1))
                need(pe, acc_init, T)
                for i in range(TI):
                    last = te.matmul(bB[:, i * E:(i + 1) * E], h2[:, i * P:(i + 1) * P], rw_sb,
                                     start=True, stop=True)
                last.then_inc(logits_done, 1)

            def transpose_comb(T):
                need_apart(pe, comb_done, T + 1)
                for i in range(TI):
                    last = te.transpose(bB[0:C_ROWS, i * P:(i + 1) * P], comb2[:, i, :], ident)
                last.then_inc(combT_done, 1)

            def bias2(T):
                need(pe, cT_done, T + 1)
                need(pe, c_row_done, T + 1)
                te.matmul(bB[:, :], b2_hi[:, :], cT[:, :], start=True, stop=False)
                te.matmul(bB[:, :], b2_lo[:, :], cT[:, :], start=False, stop=True).then_inc(b2t_done, 1)

            def finish(t):
                need(pe, acc_done, E * (t + 1))
                need(pe, h2_done, GB * (t + 2 if in_loop(t) or t < G - 1 else G))
                for i in range(TI):
                    last = te.transpose(bA[:, i * P:(i + 1) * P], acc[:, i * P:(i + 1) * P], ident)
                last.then_inc(fin_done, 1)

            def tokens(buf, T):
                return buf[:, bass.ds(T, 1), :].rearrange("p o n -> p (o n)") if in_loop(T) else buf[:, T, :]

            def product1(t, s):
                T, e, f = chunk(t, s)
                n = CH * T + s % CH
                need(pe, r_done, n - NZ + 1)
                z = zb[s % CH % NZ]
                w = slice(f * P, (f + 1) * P)
                if f == 0 and e >= STAGE:
                    need_w1_lo(pe, e)
                te.matmul(z[:, :], w1_lo[:, e, w], tokens(h2_hi, T), start=True, stop=False)
                te.matmul(z[:, :], w1_hi[:, e, w], tokens(h2_lo, T), start=False, stop=False)
                te.matmul(z[:, :], w1_hi[:, e, w], tokens(h2_hi, T), start=False, stop=True).then_inc(z_done, 1)

            def product2(t, s):
                e, f = s // FC, s % FC
                need_lo(pe, t, s)
                need_hi(pe, t, s)
                b = s % RB
                if f == 0 and e >= STAGE:
                    need_w2_lo(pe, e)
                if f == 0:
                    need(pe, yg_done, E * t + e - 1)
                y = yb[e % 2]
                te.matmul(y[:, :], w2_lo[:, e, f, :], r_hi[:, b, :], start=(f == 0), stop=False)
                te.matmul(y[:, :], w2_hi[:, e, f, :], r_lo[:, b, :], start=False, stop=False)
                te.matmul(y[:, :], w2_hi[:, e, f, :], r_hi[:, b, :], start=False, stop=(f == FC - 1)).then_inc(l2_done, 1)

            down(1)
            pe.wait_ge(M2_done, 1)
            pe.wait_ge(ones_done, 1)
            up(0)
            pe.wait_ge(subj_onehot, 1)
            pe.wait_ge(ld_style, 16)
            te.matmul(se_ps, subj_sb, oh_s[:, :], start=True, stop=True).then_inc(style_mm, 1)
            down(2)
            pe.wait_ge(style_ev, 1)
            te.matmul(hyp1_ps, hw1_sb, se_sb[:, :], start=True, stop=True).then_inc(style_mm, 1)
            down(3)
            pe.wait_ge(style_ev, 2)
            te.matmul(hyp2_ps, hw2_sb, hyp_h[:, :], start=True, stop=True).then_inc(style_mm, 1)
            pe.wait_ge(w_sel_done, 2)
            for g in range(1, G):
                last = choose(g, M_ps[1][:, (g - 1) * D:g * D])
            last.then_inc(M_done, 1)
            pe.wait_ge(style_ev, 3)
            te.matmul(sty1_ps, sw1_sb, hyp_o[:, :], start=True, stop=True).then_inc(style_mm, 1)
            pe.wait_ge(style_ev, 4)
            te.matmul(gz_ps, sw2_sb[:, 0:D], sty_h[:, :], start=True, stop=True)
            te.matmul(bz_ps, sw2_sb[:, D:2 * D], sty_h[:, :], start=True, stop=True).then_inc(style_mm, 1)
            transpose_hn(0)
            pe.wait_ge(hid_done, GB * G)
            logits(0)
            pe.wait_ge(h2lo_done, 1)
            for s in range(LEAD):
                if s % FC == 0:
                    need_w1_lo(pe, s // FC)
                product1(0, s)

            def run(t, s):
                first = not in_loop(t) and t == 0
                if not (not in_loop(t) and t == G - 1 and s + LEAD >= CH):
                    if s + LEAD == CH:
                        need(pe, h2lo_done, t + 2)
                    if first and (s + LEAD) % FC == 0:
                        need_w1_lo(pe, (s + LEAD) // FC)
                    product1(t, s + LEAD)
                if first and s % FC == 0 and s // FC < STAGE:
                    need_w2_lo(pe, s // FC)
                product2(t, s)
                if s == 0:
                    transpose_comb(t)
                if s == 0 and first:
                    pe.wait_ge(b2_done, 1)
                if s == 3:
                    bias2(t)
                if s == 4 and not (not in_loop(t) and t == 0):
                    finish(t - 1)
                if in_loop(t) and s >= SPLIT_AT:
                    if s == 8:
                        up(t + 1)
                    if s == 19:
                        transpose_hn(t + 1)
                    if s == 24:
                        logits(t + 1)
            whole(run, pe)
            finish(G - 1)


def packed(parts, widths, rows):
    import numpy as np

    at, n = widths
    a = np.zeros((rows, n), np.float32)
    for name, (c0, c1) in at.items():
        p = parts[name]
        a[0:p.shape[0], c0:c1] = p
    return a


def kernel(**inputs):
    import numpy as np
    import concourse.bacc as bacc
    from concourse.bass_utils import run_bass_kernel_spmd

    p0 = {k.removeprefix("L0_cond_"): np.asarray(v) for k, v in inputs.items()}
    q = {k.removeprefix("L1_cond_"): np.asarray(v) for k, v in inputs.items()}
    x = np.ascontiguousarray(inputs["x"])
    cols = np.zeros((P, COLS), np.float32)
    cols[:, 0:CH] = q["exp_b1"].reshape(CH, P).T
    for c, v in ((COL_LN_G, q["ln_g"]), (COL_LN_B, q["ln_b"]), (COL_HYP_B1, q["hyp_b1"]), (COL_HYP_B2, q["hyp_b2"]),
                 (COL_GAMMA_B, q["sty_b2"][0:D]), (COL_BETA_B, q["sty_b2"][D:2 * D])):
        cols[:, c] = v
    cols[0:HALF, COL_STY_B1] = q["sty_b1"]
    for j in range(GB):
        cols[HALF * j:HALF * j + A, COL_DOWN_B] = p0["down_b"]
    adapt = packed({
        "down_T": p0["down_W"].T, "up_rep": np.tile(p0["up_W"].T, (4, 1)),
        "up_ext": np.concatenate([p0["up_W"].T, p0["up_b"][None, :]]),
        "experts": p0["expert_W"].reshape(4, P, A).transpose(1, 0, 2).reshape(P, 4 * A),
        "expert_b": p0["expert_b"], "domain_emb": p0["domain_emb"], "cols": cols,
        "ident": np.eye(P, dtype=np.float32),
        "eid": np.array([[(t * P + p) // A for t in range(4)] for p in range(P)], np.float32),
        "pid": np.arange(P, dtype=np.float32)[:, None],
        "iota_e": np.tile(np.arange(E, dtype=np.float32), (P, 1)),
    }, (ADAPT, ADAPT_N), P)
    style = packed({
        "subj": q["subj_emb"], "hyp_w1": q["hyp_w1"], "hyp_w2": q["hyp_w2"], "sty_w1": q["sty_w1"],
        "sty_w2": q["sty_w2"], "router_w": q["router_w"], "ln_gamma": np.tile(p0["ln_gamma"], (P, 1)),
        "ln_beta": np.tile(p0["ln_beta"], (P, 1)), "exp_b2": np.tile(q["exp_b2"], (2, 1)),
    }, (STYLE, STYLE_N), P)
    arrays = {
        "x": x,
        "x_t": np.ascontiguousarray(x.reshape(B * S, D).T).reshape(D, G, N),
        "ids": np.tile(np.concatenate([inputs["itok_B_0_15"], inputs["itok_B_6_14"]])[None, :], (P, 1)),
        "adapt": adapt, "style": style,
        "w1": np.ascontiguousarray(q["exp_w1"].transpose(1, 0, 2)),
        "w2": np.ascontiguousarray(q["exp_w2"].reshape(E, FC, P, D).transpose(2, 0, 1, 3)),
    }
    nc = bacc.Bacc("TRN2", target_bir_lowering=False, num_devices=1)
    args = [nc.dram_tensor(k, a.shape, mybir.dt.from_np(a.dtype), kind="ExternalInput").ap() for k, a in arrays.items()]
    args.append(nc.dram_tensor("result", (B, S, D), F32, kind="ExternalOutput").ap())
    args.append(nc.dram_tensor("gates", (E, G, N), F32, kind="Internal").ap())
    program(nc, *args)
    return run_bass_kernel_spmd(nc, [arrays], core_ids=[0]).results[0]["result"]
```
